# Optimizing a Trainium2 kernel written in Bass

```python
import numpy as np
import jax
import jax.numpy as jnp

def _softmax(x, axis=-1):
    return jax.nn.softmax(x, axis=axis)

def _gelu(x):
    return jax.nn.gelu(x, approximate=True)

def _silu(x):
    return jax.nn.silu(x)

def _sigmoid(x):
    return jax.nn.sigmoid(x)

def _layernorm(x, axis=-1, eps=1e-05):
    m = jnp.mean(x, axis=axis, keepdims=True)
    v = jnp.var(x, axis=axis, keepdims=True)
    return (x - m) / jnp.sqrt(v + eps)

def _scatter_add(tgt, idx, src, axis=0):
    return tgt.at[idx].add(src)

def _segment_sum(src, seg, n):
    return jax.ops.segment_sum(src, seg, n)
kernel_name = 'mk_gnn_preln_d2_gnn_r8_71c7cb'

def setup_inputs(seed: int=0):
    np.random.seed(seed)
    _w = jnp.asarray

    def _rec_inputs():
        import jax
        import jax.numpy as jnp
        _gk = jax.random.key(seed)
        x = -0.0002928 + 1 * jax.random.normal(jax.random.fold_in(_gk, 1), (1024, 512), jnp.float32)
        src = jax.random.randint(jax.random.fold_in(_gk, 2), (16384,), 0, 1024, jnp.int32)
        dst = jnp.minimum((1024 * jax.random.uniform(jax.random.fold_in(_gk, 3), (16384,)) ** 2.0).astype(jnp.int32), 8191)
        _o = jnp.argsort(dst, stable=True)
        src = src[_o]
        dst = dst[_o]
        return (x, src, dst)
    x, src, dst = _rec_inputs()

    def _L0_gnn_setup():
        import jax, jax.numpy as jnp
        import numpy as np
        NEG = -1000000.0
        key = jax.random.key(seed)
        ks = jax.random.split(key, 8)
        N, D_IN, D_Q, D_K, E = (1024, 512, 512, 512, 32768)
        s = 1.0 / np.sqrt(D_IN)
        return {'x': jax.random.normal(ks[0], (N, D_IN), dtype=jnp.float32), 'edge_index': jax.random.randint(ks[1], (2, E), 0, N, dtype=jnp.int64), 'Wq': jax.random.normal(ks[2], (D_IN, D_Q), dtype=jnp.float32) * s, 'bq': jax.random.normal(ks[3], (D_Q,), dtype=jnp.float32) * 0.01, 'Wk': jax.random.normal(ks[4], (D_IN, D_K), dtype=jnp.float32) * s, 'bk': jax.random.normal(ks[5], (D_K,), dtype=jnp.float32) * 0.01, 'Wv': jax.random.normal(ks[6], (D_IN, D_K), dtype=jnp.float32) * s, 'bv': jax.random.normal(ks[7], (D_K,), dtype=jnp.float32) * 0.01}
    _L0_gnn_all = _L0_gnn_setup()
    _L0_gnn_in = {k: v for k, v in _L0_gnn_all.items() if k in ('Wq', 'bq', 'Wk', 'bk', 'Wv', 'bv')}
    del _L0_gnn_all

    def _L1_gnn_setup():
        import jax, jax.numpy as jnp
        import numpy as np
        N = 1250
        E = 20000
        IN_C = 512
        HID = 512
        OUT_C = 512
        BN_EPS = 1e-05
        key = jax.random.key(seed)
        ks = jax.random.split(key, 8)
        x = jax.random.normal(ks[0], (N, IN_C), dtype=jnp.float32)
        src = jax.random.randint(ks[1], (E,), 0, N)
        off = jax.random.randint(ks[2], (E,), 1, N)
        dst = (src + off) % N
        edge_index = jnp.stack([src, dst]).astype(jnp.int64)
        W1 = jax.random.normal(ks[3], (IN_C, HID), dtype=jnp.float32) * (1.0 / np.sqrt(IN_C))
        b1 = jnp.zeros((HID,), dtype=jnp.float32)
        gamma = jnp.ones((HID,), dtype=jnp.float32)
        beta = jnp.zeros((HID,), dtype=jnp.float32)
        W2 = jax.random.normal(ks[4], (HID, OUT_C), dtype=jnp.float32) * (1.0 / np.sqrt(HID))
        b2 = jnp.zeros((OUT_C,), dtype=jnp.float32)
        return {'x': x, 'W1': W1, 'b1': b1, 'gamma': gamma, 'beta': beta, 'W2': W2, 'b2': b2, 'edge_index': edge_index}
    _L1_gnn_all = _L1_gnn_setup()
    _L1_gnn_in = {k: v for k, v in _L1_gnn_all.items() if k in ('W1', 'b1', 'gamma', 'beta', 'W2', 'b2')}
    del _L1_gnn_all
    return {'x': x, 'src': src, 'dst': dst, 'L0_gnn_Wq': _L0_gnn_in['Wq'], 'L0_gnn_bq': _L0_gnn_in['bq'], 'L0_gnn_Wk': _L0_gnn_in['Wk'], 'L0_gnn_bk': _L0_gnn_in['bk'], 'L0_gnn_Wv': _L0_gnn_in['Wv'], 'L0_gnn_bv': _L0_gnn_in['bv'], 'L1_gnn_W1': _L1_gnn_in['W1'], 'L1_gnn_b1': _L1_gnn_in['b1'], 'L1_gnn_gamma': _L1_gnn_in['gamma'], 'L1_gnn_beta': _L1_gnn_in['beta'], 'L1_gnn_W2': _L1_gnn_in['W2'], 'L1_gnn_b2': _L1_gnn_in['b2']}

def reference(x, src, dst, L0_gnn_Wq, L0_gnn_bq, L0_gnn_Wk, L0_gnn_bk, L0_gnn_Wv, L0_gnn_bv, L1_gnn_W1, L1_gnn_b1, L1_gnn_gamma, L1_gnn_beta, L1_gnn_W2, L1_gnn_b2):
    import jax
    import jax.numpy as jnp

    def _L0_gnn_ref(x, edge_index, Wq, bq, Wk, bk, Wv, bv):
        import jax, jax.numpy as jnp
        import numpy as np
        NEG = -1000000.0
        q = x @ Wq + bq
        k = x @ Wk + bk
        v = x @ Wv + bv
        N = x.shape[0]
        adj = jnp.zeros((N, N), dtype=x.dtype).at[edge_index[0], edge_index[1]].set(1.0)
        a = q @ k.T / jnp.sqrt(jnp.asarray(q.shape[-1], dtype=x.dtype))
        a = a * adj + (1.0 - adj) * NEG
        attn = jax.nn.softmax(a, axis=-1)
        return attn @ v

    def _L1_gnn_ref(x, W1, b1, gamma, beta, W2, b2, edge_index):
        import jax, jax.numpy as jnp
        import numpy as np
        N = 1250
        E = 20000
        IN_C = 512
        HID = 512
        OUT_C = 512
        BN_EPS = 1e-05
        n = x.shape[0]
        loops = jnp.arange(n, dtype=edge_index.dtype)
        src = jnp.concatenate([edge_index[0], loops])
        dst = jnp.concatenate([edge_index[1], loops])
        deg = jax.ops.segment_sum(jnp.ones_like(dst, dtype=x.dtype), dst, num_segments=n)
        dinv = jnp.where(deg > 0, deg ** (-0.5), 0.0)
        w = dinv[src] * dinv[dst]

        def agg(h):
            return jax.ops.segment_sum(w[:, None] * h[dst], src, num_segments=n)
        h = x @ W1 + b1
        h = agg(h)
        mu = jnp.mean(h, axis=0)
        var = jnp.var(h, axis=0)
        h = gamma * (h - mu) * jax.lax.rsqrt(var + BN_EPS) + beta
        h = jax.nn.relu(h)
        h = h @ W2 + b2
        h = agg(h)
        return h
    edge_index = jnp.stack([src, dst])
    h = jnp.maximum(_layernorm(x, axis=-1), 0.0)
    x = x + _L0_gnn_ref(h, edge_index, L0_gnn_Wq, L0_gnn_bq, L0_gnn_Wk, L0_gnn_bk, L0_gnn_Wv, L0_gnn_bv)
    h = jnp.maximum(_layernorm(x, axis=-1), 0.0)
    x = x + _L1_gnn_ref(h, L1_gnn_W1, L1_gnn_b1, L1_gnn_gamma, L1_gnn_beta, L1_gnn_W2, L1_gnn_b2, edge_index)
    return x

_drawn_inputs = setup_inputs


def setup_inputs(seed=0):
    import zlib

    import numpy as np

    out = dict(_drawn_inputs(seed))
    spreads = {'L1_gnn_b1': (0.0, 0.1),
     'L1_gnn_gamma': (1.0, 0.2),
     'L1_gnn_beta': (0.0, 0.1),
     'L1_gnn_b2': (0.0, 0.1)}
    factors = {'L0_gnn_bq': 64.0, 'L0_gnn_bk': 64.0, 'L0_gnn_bv': 6.618}
    for name, (base, spread) in spreads.items():
        noise = np.random.default_rng([zlib.crc32(name.encode()), seed]).standard_normal(out[name].shape)
        drawn = base * np.exp(spread * noise) if base else spread * noise
        out[name] = jnp.asarray(drawn.astype(out[name].dtype))
    for name, factor in factors.items():
        out[name] = (out[name] * factor).astype(out[name].dtype)
    return out
```

```python
from contextlib import ExitStack

import concourse.bass as bass
from concourse import mybir

P = 128
N = 1024
D = 512
E = 16384
NT = N // P
KC = D // P
NCH = E // P
HALF = 512
RING = 8
STAGE_K = 2
EXACT = 4096.0
SCALE = float(D) ** -0.5
NEG = -1.0e6
EPS = 1e-5

ALU = mybir.AluOpType
ACT = mybir.ActivationFunctionType
AX = mybir.AxisListType
F32 = mybir.dt.float32
F32R = mybir.dt.float32r
BF16 = mybir.dt.bfloat16
F16 = mybir.dt.float16
I32 = mybir.dt.int32
I16 = mybir.dt.int16
U8 = mybir.dt.uint8


def gnn_kernel(nc, x, src, dst, Wq, bq, Wk, bk, Wv, bv, W1, b1, gamma, beta, W2, b2, out):
    ctx = ExitStack()

    def sb(name, shape, dt, where=ctx):
        return where.enter_context(nc.sbuf_tensor(name, shape, dt))

    def shared(*groups):
        made = []
        for g in groups:
            s = ExitStack()
            made += [sb(name, shape, dt, s) for name, shape, dt in g]
            s.close()
        return made

    def hold(name, kib):
        sb(name, [P, 256 * kib], F32)

    hT, pT, w2, g32 = shared(
        [("hT", [P, 2, KC, N], F32R)],
        [("pT", [P, 2, 2, NT, P], F32R), ("w2", [P, 2, KC, D], F32R)],
        [("g32", [P, KC, N], F32)])
    hold("region_hT", 32)
    wA, x1 = shared([("wA", [P, 2, KC, D], F32R)], [("x1", [P, NT, D], F32)])
    hold("region_wA", 16)
    wB = sb("wB", [P, 2, KC, D], F32R)
    qh, src_oh, dst_oh, adjT, iota, edge_i, edge_f, ecol = shared(
        [("qh", [P, NT, 2, KC * P], F32R)],
        [("src_oh", [P, RING, N], BF16), ("dst_oh", [P, RING, P], BF16), ("adjT", [P, 2, N], BF16),
         ("iota", [P, N], F16), ("edge_i", [P, 2, P], I32), ("edge_f", [P, 2, P], F32),
         ("ecol", [P, 2, NCH], F32)])
    hold("region_qh", 32)
    kT, cnt = shared([("kT", [P, 2, KC, N], F32R)], [("cnt", [P, NT, N], F32R)])
    hold("region_kT", 32)
    v, zT = shared([("v", [P, NT, 2, D], F32R)], [("zT", [P, 2, KC, N], F32R)])
    hold("region_v", 32)
    T = sb("T", [P, 2, N], F32)
    stage = sb("stage", [P, STAGE_K, D], F32)
    cnt16 = sb("cnt16", [P, NT, N], I16)
    adj = sb("adj", [P, NT, N], U8)
    xt = sb("xt", [P, 2, D], F32)
    ht = sb("ht", [P, D], F32)
    hnT, res, res_h = shared([("hnT", [P, 2, KC * P], F32R)],
                             [("res", [P, HALF], F32R), ("res_h", [P, 2, P], F32R)])
    hold("region_hnT", 4)
    vb = sb("vb", [P, 2, D], F32)
    bias_row = sb("bias_row", [P, 2, D], F32)
    ident = sb("ident", [P, P], F32)
    identb = sb("identb", [P, P], BF16)
    zerob = sb("zerob", [P, P], BF16)
    ones = sb("ones", [P, P], F32)
    half_pow = sb("half_pow", [P, NT], F32)
    bcol = sb("bcol", [P, 4, KC], F32)
    lohi = sb("lohi", [1, 2 * NT], I32)
    blk0 = sb("blk0", [P, NT], F32)
    chunk1 = sb("chunk1", [P, 2], F32)
    ext = sb("ext", [P, 2], F32)
    hit = sb("hit", [P, 3, NT], F32)
    span = sb("span", [P, 2, NT], F32)
    spanr = sb("spanr", [P, 2, NT], F32)
    lim = sb("lim", [P, 2, NT], F32)
    lsum = sb("lsum", [P, 4, NT], F32)
    lnc = sb("lnc", [P, 6, NT], F32)
    deg = sb("deg", [P, NT], F32)
    dinv = sb("dinv", [P, NT], F32)
    degm = sb("degm", [P, 4], F32)
    flag = sb("flag", [1, 1], I32)
    smx = sb("smx", [P, 4, NT], F32)
    bnst = sb("bnst", [P, 2, 6], F32)
    bnag = sb("bnag", [P, NT, 2], F32)
    bnc = sb("bnc", [P, 4, KC], F32)
    lnb = sb("lnb", [P, 4, NT], F32)

    ps = ctx.enter_context(nc.psum_tensor("ps", [P, 8, HALF], F32))
    bank = lambda b: ps[:, b, :]

    sem_names = """consts edges_in x_in0 x_in1 w_in stage_hi stage_lo bcol_in bias_in b1_in
    edge_f_ready ecol_ps ecol_ready span_ready span_max bounds_ready onehots onehots_used c_done c16
    adjT_ready adj_ps adj_evac  dinv_ready ln_sum ln_mean ln_sq ln_coef h_ready hT_ps hT_hi hT_lo
    q_ps kq_hi kq_lo v_ps v_tmp v_hi v_lo s_ps mask_set masked top_ready exp_done rinv_ready pT_ps p_hi p_lo
    pv_ps x1_ready bn_ready ln2_coef h2_ready h2T_ps h2T_hi h2T_lo w1_ps h1_tmp h1_hi h1_lo
    diag_ready bc_ps bc_ready cnt_ready agg1_ps g_ready gstat z_coef z_ready z_hi z_lo w2_ps h2b_tmp h2b_hi h2b_lo
    agg2_ps out_ready out_done0 out_done1 small pool_small flag_max flag_ready res_ready res_used vb_small""".split()
    S = {n: ctx.enter_context(nc.semaphore(n)) for n in sem_names}

    weights = [(Wk, wA), (Wv, wB), (Wq, wA), (W1, wB), (W2, w2)]
    LOADS = KC // STAGE_K

    block = ctx.enter_context(nc.Block())

    @block.sync
    def _(sp):
        sp.dma_start(edge_i[:, 0, :], dst.rearrange("(c j) -> c j", j=P)).then_inc(S["edges_in"], 16)
        sp.dma_start(edge_i[:, 1, :], src.rearrange("(c j) -> c j", j=P)).then_inc(S["edges_in"], 16)

        def load_x(n):
            if 2 <= n < NT + 2:
                sp.wait_ge(S["h_ready"], n - 1)
            if n >= NT + 2:
                sp.wait_ge(S["x1_ready"], n - NT - 1)
            sp.dma_start(xt[:, n % 2, :], x[(n % NT) * P:(n % NT + 1) * P, :]).then_inc(S[f"x_in{n % 2}"], 16)

        def load_w(i):
            w, _ = weights[i]
            for j in range(LOADS):
                n = i * LOADS + j
                if n:
                    sp.wait_ge(S["stage_hi"], n)
                    sp.wait_ge(S["stage_lo"], n)
                sp.dma_start(stage[:, :, :], w.rearrange("(k p) n -> p k n", p=P)[
                    :, j * STAGE_K:(j + 1) * STAGE_K, :]).then_inc(S["w_in"], 16)

        load_x(0)
        load_x(1)
        for i, b in enumerate((bq, bk, gamma, beta)):
            sp.dma_start(bcol[:, i, :], b.rearrange("(c p) -> p c", p=P),
                         allow_slow_non_contiguous=True).then_inc(S["bcol_in"], 16)
        sp.dma_start(bias_row[:, 0, :], bv.rearrange("(o n) -> o n", o=1).to_broadcast([P, D])).then_inc(S["bias_in"], 16)
        sp.dma_start(bias_row[:, 1, :], b1.rearrange("(o n) -> o n", o=1).to_broadcast([P, D])).then_inc(S["b1_in"], 16)
        for t in range(2, NT):
            load_x(t)
            if t == 3:
                load_w(0)
            if t == 6:
                load_w(1)
        load_w(2)
        for t in range(2):
            load_x(NT + t)
        load_w(3)
        load_w(4)
        sp.wait_ge(S["v_tmp"], NT)
        sp.dma_start(bias_row[:, 0, :], b2.rearrange("(o n) -> o n", o=1).to_broadcast([P, D])).then_inc(S["bias_in"], 16)
        for t in range(2, NT):
            load_x(NT + t)
        for t in range(NT):
            sp.wait_ge(S["out_ready"], t + 1)
            sp.dma_start(out[t * P:(t + 1) * P, :], xt[:, t % 2, :]).then_inc(S[f"out_done{t % 2}"], 16)
        for u in range(2):
            sp.wait_ge(S[f"out_done{u}"], 16 * NT // 2)

    @block.gpsimd
    def _(pool):
        def pw(out_, in_, w):
            return pool.tensor_tensor(out_, in_, half_pow[:, 0:w], ALU.pow)

        pool.memset(ident[:, :], 0.0).then_inc(S["small"], 1)
        pool.iota(blk0[:, :], pattern=[[P, NT]], base=0, channel_multiplier=0,
                  allow_small_or_imprecise_dtypes=True)
        pool.iota(chunk1[:, 0:1], pattern=[[0, 1]], base=1, channel_multiplier=1,
                  allow_small_or_imprecise_dtypes=True)
        pool.iota(chunk1[:, 1:2], pattern=[[0, 1]], base=NCH, channel_multiplier=-1,
                  allow_small_or_imprecise_dtypes=True)
        pool.wait_ge(S["small"], 1)
        pool.affine_select(out=ident[:, :], in_=ident[:, :], compare_op=ALU.not_equal, fill=1.0, base=0,
                           pattern=[[-1, P]], channel_multiplier=1).then_inc(S["consts"], 1)
        pool.iota(iota[:, :], pattern=[[1, N]], base=0, channel_multiplier=0,
                  allow_small_or_imprecise_dtypes=True).then_inc(S["consts"], 1)
        pool.wait_ge(S["consts"], 1)
        pool.tensor_copy(identb[:, :], ident[:, :])
        pool.memset(half_pow[:, :], -0.5)
        pool.memset(ones[:, :], 1.0)
        pool.memset(zerob[:, :], 0.0).then_inc(S["consts"], 1)

        pool.wait_ge(S["span_ready"], 1)
        pool.partition_all_reduce(spanr[:, :, :].rearrange("p a b -> p (a b)"),
                                  span[:, :, :].rearrange("p a b -> p (a b)"), P,
                                  bass.bass_isa.ReduceOp.max).then_inc(S["span_max"], 1)

        n_small = [0]

        def step(ins):
            n_small[0] += 1
            ins.then_inc(S["pool_small"], 1)
            pool.wait_ge(S["pool_small"], n_small[0])

        def ln1_mean(t):
            pool.wait_ge(S["ln_sum"], t + 1)
            pool.tensor_scalar(lnc[:, 0, t:t + 1], lsum[:, 0, t:t + 1], -1.0 / D, 0.0, ALU.mult,
                               ALU.add).then_inc(S["ln_mean"], 1)

        def ln1_coef(t):
            pool.wait_ge(S["ln_sq"], t + 1)
            step(pool.tensor_scalar(lnc[:, 1, t:t + 1], lsum[:, 1, t:t + 1], 1.0 / D, EPS, ALU.mult, ALU.add))
            step(pw(lnc[:, 2, t:t + 1], lnc[:, 1, t:t + 1], 1))
            pool.tensor_tensor(lnc[:, 3, t:t + 1], lnc[:, 0, t:t + 1], lnc[:, 2, t:t + 1],
                               ALU.mult).then_inc(S["ln_coef"], 1)

        def split_w(i):
            _, w = weights[i]
            for j in range(LOADS):
                n = i * LOADS + j
                ks = slice(j * STAGE_K, (j + 1) * STAGE_K)
                pool.wait_ge(S["stage_hi"], n + 1)
                pool.tensor_tensor(w[:, 1, ks, :], stage[:, :, :], w[:, 0, ks, :].bitcast(F32),
                                   ALU.subtract).then_inc(S["stage_lo"], 1)

        for t in range(NT):
            ln1_mean(t)
            ln1_coef(t)
            if t == 3:
                split_w(0)
            if t == 6:
                split_w(1)
        pool.wait_ge(S["flag_max"], 1)
        pw(dinv[:, :], deg[:, :], NT).then_inc(S["dinv_ready"], 1)
        pool.partition_all_reduce(degm[:, 2:3], degm[:, 1:2], P,
                                  bass.bass_isa.ReduceOp.max).then_inc(S["flag_max"], 1)
        for t in range(NT):
            if t == 1:
                split_w(2)
            pool.wait_ge(S["v_hi"], t + 1)
            pool.tensor_tensor(v[:, t, 1, :], vb[:, t % 2, :], v[:, t, 0, :].bitcast(F32),
                               ALU.subtract).then_inc(S["v_lo"], 1)
        split_w(3)

        def mask_fill(t):
            if t >= 2:
                pool.wait_ge(S["pT_ps"], t - 1)
            pool.memset(T[:, t % 2, :], NEG / SCALE).then_inc(S["mask_set"], 1)

        def ln2_coef(t):
            pool.wait_ge(S["bn_ready"], t + 1)
            step(pool.tensor_scalar(lnb[:, 0, t:t + 1], bnag[:, t, 1:2], 1.0, EPS, ALU.mult, ALU.add))
            step(pw(lnb[:, 1, t:t + 1], lnb[:, 0, t:t + 1], 1))
            step(pool.tensor_scalar(lnb[:, 2, t:t + 1], bnag[:, t, 0:1], -1.0, 0.0, ALU.mult, ALU.add))
            pool.tensor_tensor(lnb[:, 3, t:t + 1], lnb[:, 2, t:t + 1], lnb[:, 1, t:t + 1],
                               ALU.mult).then_inc(S["ln2_coef"], 1)

        mask_fill(0)
        mask_fill(1)
        split_w(4)
        for t in range(NT):
            ln2_coef(t)
            if t + 2 < NT:
                mask_fill(t + 2)
        for c in range(KC):
            pool.wait_ge(S["gstat"], c + 1)
            step(pool.tensor_scalar(bnc[:, 0, c:c + 1], bnag[:, c, 1:2], 1.0, EPS, ALU.mult, ALU.add))
            step(pw(bnc[:, 1, c:c + 1], bnc[:, 0, c:c + 1], 1))
            if c == 0:
                pool.wait_ge(S["bcol_in"], 64)
            step(pool.tensor_tensor(bnc[:, 2, c:c + 1], bnc[:, 1, c:c + 1], bcol[:, 2, c:c + 1], ALU.mult))
            step(pool.tensor_tensor(bnc[:, 0, c:c + 1], bnag[:, c, 0:1], bnc[:, 2, c:c + 1], ALU.mult))
            pool.tensor_tensor(bnc[:, 3, c:c + 1], bcol[:, 3, c:c + 1], bnc[:, 0, c:c + 1],
                               ALU.subtract).then_inc(S["z_coef"], 1)

    @block.scalar
    def _(act):
        def split_w(i):
            _, w = weights[i]
            for j in range(LOADS):
                n = i * LOADS + j
                act.wait_ge(S["w_in"], 16 * (n + 1))
                act.activation(w[:, 0, j * STAGE_K:(j + 1) * STAGE_K, :], stage[:, :, :],
                               ACT.Copy).then_inc(S["stage_hi"], 1)

        def hT_hi(t):
            act.wait_ge(S["hT_ps"], t + 1)
            act.activation(hT[:, 0, :, t * P:(t + 1) * P],
                           bank(4 + t % 2).rearrange("p (k n) -> p k n", k=KC), ACT.Copy).then_inc(S["hT_hi"], 1)

        def adj_out(b):
            act.wait_ge(S["adj_ps"], b + 1)
            act.activation(adj[:, :, b * P:(b + 1) * P],
                           bank(6 + b % 2).bitcast(BF16).rearrange("p (s n) -> p s n", s=NT),
                           ACT.Copy).then_inc(S["adj_evac"], 1)

        for t in range(NT):
            act.wait_ge(S[f"x_in{t % 2}"], 16 * (t // 2 + 1))
            if t >= 1:
                act.wait_ge(S["hT_ps"], t)
            act.activation(ht[:, :], xt[:, t % 2, :], ACT.Copy,
                           accum_out=lsum[:, 0, t:t + 1]).then_inc(S["ln_sum"], 1)
            if t >= 2:
                adj_out(t - 2)
            act.wait_ge(S["ln_mean"], t + 1)
            act.activation(ht[:, :], xt[:, t % 2, :], ACT.Square, bias=lnc[:, 0, t:t + 1],
                           accum_out=lsum[:, 1, t:t + 1]).then_inc(S["ln_sq"], 1)
            if t >= 1:
                hT_hi(t - 1)
            act.wait_ge(S["ln_coef"], t + 1)
            act.activation(ht[:, :], xt[:, t % 2, :], ACT.Relu, bias=lnc[:, 3, t:t + 1],
                           scale=lnc[:, 2, t:t + 1]).then_inc(S["h_ready"], 1)
            act.wait_ge(S["c_done"], t + 1)
            act.activation(cnt16[:, t, :], ps[:, 2 * (t % 2):2 * (t % 2) + 2, :].rearrange("p a n -> p (a n)"),
                           ACT.Copy, accum_out=deg[:, t:t + 1]).then_inc(S["c16"], 1)
            if t == 3:
                split_w(0)
            if t == 6:
                split_w(1)
        hT_hi(NT - 1)
        adj_out(NT - 2)
        adj_out(NT - 1)

        def kq_hi(g, dest, bias):
            act.wait_ge(S["q_ps"], g + 1)
            act.activation(dest, bank(4 + g % 4), ACT.Identity, bias=bias).then_inc(S["kq_hi"], 1)

        act.wait_ge(S["bcol_in"], 64)
        for g in range(2 * KC):
            n, c = divmod(g, KC)
            kq_hi(g, kT[:, 0, c, n * HALF:(n + 1) * HALF], bcol[:, 1, c:c + 1])
        for t in range(NT):
            if t == 1:
                act.wait_ge(S["q_ps"], 2 * KC)
                split_w(2)
            act.wait_ge(S["v_tmp"], t + 1)
            act.activation(v[:, t, 0, :], vb[:, t % 2, :], ACT.Copy).then_inc(S["v_hi"], 1)
        for g in range(2 * KC):
            n, c = divmod(g, KC)
            kq_hi(2 * KC + g, qh[:, 4 * n:4 * n + 4, 0, c * P:(c + 1) * P], bcol[:, 0, c:c + 1])
        act.wait_ge(S["v_ps"], NT)
        split_w(3)
        act.wait_ge(S["q_ps"], 4 * KC)
        split_w(4)

        def softmax_exp(t):
            act.wait_ge(S["top_ready"], t + 1)
            act.activation(T[:, t % 2, :], T[:, t % 2, :], ACT.Exp, bias=smx[:, 1, t:t + 1], scale=SCALE,
                           accum_out=smx[:, 2, t:t + 1]).then_inc(S["exp_done"], 1)

        def p_hi(t):
            act.wait_ge(S["pT_ps"], t + 1)
            if t >= 2:
                act.wait_ge(S["pv_ps"], t - 1)
            act.activation(pT[:, t % 2, 0, :, :], ps[:, 4:6, :].rearrange("p a (k n) -> p (a k) n", n=P),
                           ACT.Copy).then_inc(S["p_hi"], 1)

        def h2_relu(t):
            act.wait_ge(S["ln2_coef"], t + 1)
            if t >= 1:
                act.wait_ge(S["h2T_ps"], t)
            act.activation(ht[:, :], x1[:, t, :], ACT.Relu, bias=lnb[:, 3, t:t + 1],
                           scale=lnb[:, 1, t:t + 1]).then_inc(S["h2_ready"], 1)

        def h2T_hi(t):
            act.wait_ge(S["h2T_ps"], t + 1)
            if t >= 1:
                act.wait_ge(S["w1_ps"], t)
            act.activation(hnT[:, 0, :], bank(7), ACT.Copy).then_inc(S["h2T_hi"], 1)

        def h1_hi(t):
            act.wait_ge(S["h1_tmp"], t + 1)
            act.activation(qh[:, t, 0, :], vb[:, t % 2, :], ACT.Copy, scale=dinv[:, t:t + 1]).then_inc(S["h1_hi"], 1)

        act.wait_ge(S["dinv_ready"], 1)
        for i in range(NT + 2):
            if i >= 2:
                h2_relu(i - 2)
                h2T_hi(i - 2)
            if 1 <= i <= NT:
                p_hi(i - 1)
            if i < NT:
                softmax_exp(i)
            if i >= 2:
                h1_hi(i - 2)
        act.wait_ge(S["s_ps"], NT)
        for b in range(NT):
            act.activation(cnt[:, b, :], cnt16[:, b, :], ACT.Copy).then_inc(S["cnt_ready"], 1)
        act.wait_ge(S["bc_ps"], 1)
        act.activation(T[:, 1, :], ps[:, 0:2, :].rearrange("p a n -> p (a n)"), ACT.Copy).then_inc(S["bc_ready"], 1)
        for c in range(KC):
            act.wait_ge(S["z_coef"], c + 1)
            act.activation(g32[:, c, :], g32[:, c, :], ACT.Relu, bias=bnc[:, 3, c:c + 1],
                           scale=bnc[:, 2, c:c + 1]).then_inc(S["z_ready"], 1)
            act.wait_ge(S["z_ready"], c + 1)
            act.activation(zT[:, 0, c, :], g32[:, c, :], ACT.Copy).then_inc(S["z_hi"], 1)
        for t in range(NT):
            act.wait_ge(S["h2b_tmp"], t + 1)
            act.activation(qh[:, t, 0, :], vb[:, t % 2, :], ACT.Copy, scale=dinv[:, t:t + 1]).then_inc(S["h2b_hi"], 1)

    @block.vector
    def _(dve):
        n_small = [0]

        def step(ins):
            n_small[0] += 1
            ins.then_inc(S["vb_small"], 1)
            dve.wait_ge(S["vb_small"], n_small[0])

        dve.wait_ge(S["edges_in"], 32)
        dve.tensor_copy(edge_f[:, :, :], edge_i[:, :, :]).then_inc(S["edge_f_ready"], 1)
        dve.wait_ge(S["edge_f_ready"], 1)
        dve.tensor_reduce(ext[:, 0:1], edge_f[:, 0, :], AX.X, ALU.min)
        step(dve.tensor_reduce(ext[:, 1:2], edge_f[:, 0, :], AX.X, ALU.max))
        dve.wait_ge(S["consts"], 3)
        dve.tensor_scalar(hit[:, 0, :], blk0[:, :], ext[:, 1:2], None, ALU.is_le)
        step(dve.tensor_scalar(hit[:, 1, :], blk0[:, :], float(P - 1), ext[:, 0:1], ALU.add, ALU.is_ge))
        step(dve.tensor_tensor(hit[:, 2, :], hit[:, 0, :], hit[:, 1, :], ALU.mult))
        dve.tensor_scalar(span[:, 0, :], hit[:, 2, :], chunk1[:, 0:1], None, ALU.mult)
        dve.tensor_scalar(span[:, 1, :], hit[:, 2, :], chunk1[:, 1:2], None, ALU.mult).then_inc(S["span_ready"], 1)
        dve.wait_ge(S["ecol_ps"], 1)
        dve.tensor_copy(ecol[:, :, :], bank(6)[:, 0:2 * P].rearrange("p (a n) -> p a n", a=2)).then_inc(S["ecol_ready"], 1)
        dve.wait_ge(S["span_max"], 1)
        step(dve.tensor_scalar(lim[0:1, 0, :], spanr[0:1, 1, :], -1.0, float(NCH), ALU.mult, ALU.add))
        step(dve.tensor_scalar(lim[0:1, 0, :], lim[0:1, 0, :], float(NCH - 1), None, ALU.min))
        step(dve.scalar_tensor_tensor(out=lim[0:1, 1, :], in0=lim[0:1, 0, :], scalar=1.0, in1=spanr[0:1, 0, :],
                                      op0=ALU.add, op1=ALU.max))
        dve.tensor_copy(lohi[0:1, :], lim[0:1, :, :].rearrange("p a b -> p (a b)")).then_inc(S["bounds_ready"], 1)
        dve.wait_ge(S["bounds_ready"], 1)
        dve.wait_ge(S["ecol_ready"], 1)

        def adj_cols(b):
            dve.wait_ge(S["c16"], b + 1)
            if b >= 2:
                dve.wait_ge(S["adj_ps"], b - 1)
            dve.tensor_scalar(adjT[:, b % 2, :], cnt16[:, b, :], 1.0, None, ALU.min).then_inc(S["adjT_ready"], 1)
            dve.wait_ge(S["adjT_ready"], b + 1)
            dve.tensor_tensor(cnt16[:, b, b * P:(b + 1) * P], cnt16[:, b, b * P:(b + 1) * P], identb[:, :], ALU.add)

        def hT_lo(t):
            dve.wait_ge(S["hT_hi"], t + 1)
            dve.tensor_tensor(hT[:, 1, :, t * P:(t + 1) * P], bank(4 + t % 2).rearrange("p (k n) -> p k n", k=KC),
                              hT[:, 0, :, t * P:(t + 1) * P].bitcast(F32), ALU.subtract).then_inc(S["hT_lo"], 1)

        made = dve.alloc_register("made")
        dve.reg_mov(made, 0)
        for b in range(NT):
            first = dve.value_load(lohi[0:1, b:b + 1], min_val=0, max_val=NCH - 1)
            end = dve.value_load(lohi[0:1, NT + b:NT + b + 1], min_val=1, max_val=NCH)
            with dve.Fori(first, end) as c:
                k = dve.snap(made, min_val=0, max_val=NT * NCH)
                slot = k & (RING - 1)
                dve.wait_ge(S["onehots_used"], k + 1)
                dve.tensor_scalar(src_oh[:, bass.ds(slot, 1), :].rearrange("p a n -> p (a n)"), iota[:, :],
                                  ecol[:, 1, bass.ds(c, 1)], None, ALU.is_equal)
                dve.tensor_scalar(dst_oh[:, bass.ds(slot, 1), :].rearrange("p a n -> p (a n)"),
                                  iota[:, b * P:(b + 1) * P], ecol[:, 0, bass.ds(c, 1)], None,
                                  ALU.is_equal).then_inc(S["onehots"], 1)
                dve.reg_add(made, made, 1)
            if b >= 1:
                adj_cols(b - 1)
                hT_lo(b - 1)
        adj_cols(NT - 1)
        hT_lo(NT - 1)
        step(dve.tensor_scalar(deg[:, :], deg[:, :], 1.0, None, ALU.add))
        dve.tensor_reduce(degm[:, 1:2], deg[:, :], AX.X, ALU.max).then_inc(S["flag_max"], 1)
        dve.wait_ge(S["flag_max"], 1)
        dve.wait_ge(S["flag_max"], 2)
        step(dve.tensor_scalar(degm[0:1, 3:4], degm[0:1, 2:3], EXACT, None, ALU.is_gt))
        dve.tensor_copy(flag[0:1, 0:1], degm[0:1, 3:4]).then_inc(S["flag_ready"], 1)

        def kq_lo(g, dest, hi, bias, parts=None):
            dve.wait_ge(S["kq_hi"], g + 1)
            src_ = bank(4 + g % 4)
            if parts:
                src_ = src_.rearrange("p (t n) -> p t n", t=parts)
            dve.scalar_tensor_tensor(out=dest, in0=src_, scalar=bias, in1=hi.bitcast(F32), op0=ALU.add,
                                     op1=ALU.subtract).then_inc(S["kq_lo"], 1)

        for g in range(2 * KC):
            n, c = divmod(g, KC)
            kq_lo(g, kT[:, 1, c, n * HALF:(n + 1) * HALF], kT[:, 0, c, n * HALF:(n + 1) * HALF], bcol[:, 1, c:c + 1])
        dve.wait_ge(S["bias_in"], 16)
        for t in range(NT):
            dve.wait_ge(S["v_ps"], t + 1)
            if t >= 2:
                dve.wait_ge(S["v_lo"], t - 1)
            dve.tensor_tensor(vb[:, t % 2, :], bank(t % 4), bias_row[:, 0, :], ALU.add).then_inc(S["v_tmp"], 1)
        for g in range(2 * KC):
            n, c = divmod(g, KC)
            at = lambda part: qh[:, 4 * n:4 * n + 4, part, c * P:(c + 1) * P]
            kq_lo(2 * KC + g, at(1), at(0), bcol[:, 0, c:c + 1], parts=4)

        def mask_and_max(t):
            dve.wait_ge(S["mask_set"], t + 1)
            dve.wait_ge(S["s_ps"], t + 1)
            dve.copy_predicated(T[:, t % 2, :], adj[:, t, :],
                                ps[:, 2 * (t % 2):2 * (t % 2) + 2, :].rearrange("p a n -> p (a n)")
                                ).then_inc(S["masked"], 1)
            dve.wait_ge(S["masked"], t + 1)
            step(dve.tensor_reduce(smx[:, 0, t:t + 1], T[:, t % 2, :], AX.X, ALU.max))
            dve.tensor_scalar(smx[:, 1, t:t + 1], smx[:, 0, t:t + 1], -SCALE, None, ALU.mult).then_inc(S["top_ready"], 1)

        def p_lo(t):
            dve.wait_ge(S["p_hi"], t + 1)
            dve.tensor_tensor(pT[:, t % 2, 1, :, :], ps[:, 4:6, :].rearrange("p a (k n) -> p (a k) n", n=P),
                              pT[:, t % 2, 0, :, :].bitcast(F32), ALU.subtract).then_inc(S["p_lo"], 1)
            dve.wait_ge(S["exp_done"], t + 1)
            dve.reciprocal(smx[:, 3, t:t + 1], smx[:, 2, t:t + 1]).then_inc(S["rinv_ready"], 1)

        def residual(t):
            n = NT + t
            dve.wait_ge(S[f"x_in{n % 2}"], 16 * (n // 2 + 1))
            dve.wait_ge(S["rinv_ready"], t + 1)
            dve.wait_ge(S["pv_ps"], t + 1)
            dve.scalar_tensor_tensor(out=x1[:, t, :], in0=bank(6), scalar=smx[:, 3, t:t + 1], in1=xt[:, n % 2, :],
                                     op0=ALU.mult, op1=ALU.add).then_inc(S["x1_ready"], 1)
            dve.wait_ge(S["x1_ready"], t + 1)
            step(dve.bn_stats(bnst[:, 0, :], x1[:, t, :]))
            dve.bn_aggr(bnag[:, t, :], bnst[:, 0:1, :]).then_inc(S["bn_ready"], 1)
            dve.wait_ge(S["bn_ready"], t + 1)

        def h2T_lo(t):
            dve.wait_ge(S["h2T_hi"], t + 1)
            dve.tensor_tensor(hnT[:, 1, :], bank(7), hnT[:, 0, :].bitcast(F32), ALU.subtract).then_inc(S["h2T_lo"], 1)

        def h1_out(t):
            dve.wait_ge(S["w1_ps"], t + 1)
            dve.tensor_tensor(vb[:, t % 2, :], bank(7), bias_row[:, 1, :], ALU.add).then_inc(S["h1_tmp"], 1)
            dve.wait_ge(S["h1_hi"], t + 1)
            dve.scalar_tensor_tensor(out=qh[:, t, 1, :], in0=vb[:, t % 2, :], scalar=dinv[:, t:t + 1],
                                     in1=qh[:, t, 0, :].bitcast(F32), op0=ALU.mult,
                                     op1=ALU.subtract).then_inc(S["h1_lo"], 1)

        dve.wait_ge(S["b1_in"], 16)
        for i in range(NT + 2):
            if i >= 2:
                h2T_lo(i - 2)
            if 1 <= i <= NT:
                p_lo(i - 1)
            if i < NT:
                mask_and_max(i)
            if i >= 2:
                h1_out(i - 2)
            if 1 <= i <= NT:
                residual(i - 1)
        def z_lo(c):
            dve.wait_ge(S["z_hi"], c + 1)
            dve.tensor_tensor(zT[:, 1, c, :], g32[:, c, :], zT[:, 0, c, :].bitcast(F32),
                              ALU.subtract).then_inc(S["z_lo"], 1)

        for b in range(NT):
            ins = dve.tensor_scalar(T[:, 0, b * P:(b + 1) * P], ident[:, :], dinv[:, b:b + 1], None, ALU.mult)
        ins.then_inc(S["diag_ready"], 1)
        dve.wait_ge(S["flag_ready"], 1)
        large = dve.value_load(flag[0:1, 0:1], min_val=0, max_val=1)

        def rest_of_counts(g, cols, h_cols=None):
            with dve.If(large > 0):
                with dve.Fori(0, NT) as d:
                    dve.wait_ge(S["res_used"], d + g * NT + 1)
                    w = cols.stop - cols.start
                    if h_cols:
                        dve.tensor_copy(res_h[:, :, :], qh[:, bass.ds(d, 1), :, h_cols].rearrange(
                            "p t a n -> p (t a) n").bitcast(F32))
                    dve.tensor_tensor(res[:, 0:w], cnt16[:, bass.ds(d, 1), cols].rearrange("p t n -> p (t n)"),
                                      cnt[:, bass.ds(d, 1), cols].rearrange("p t n -> p (t n)").bitcast(F32),
                                      ALU.subtract).then_inc(S["res_ready"], 1)

        dve.wait_ge(S["cnt_ready"], NT)
        dve.wait_ge(S["bc_ready"], 1)
        for c in range(KC):
            for n in range(2):
                g = 2 * c + n
                rest_of_counts(g, slice(n * HALF, (n + 1) * HALF), slice(c * P, (c + 1) * P))
                dve.wait_ge(S["agg1_ps"], g + 1)
                dve.tensor_tensor(g32[:, c, n * HALF:(n + 1) * HALF], bank(g % 4 + 2),
                                  T[:, 1, n * HALF:(n + 1) * HALF], ALU.mult).then_inc(S["g_ready"], 1)
                dve.wait_ge(S["g_ready"], g + 1)
                step(dve.bn_stats(bnst[:, n, :], g32[:, c, n * HALF:(n + 1) * HALF]))
            dve.bn_aggr(bnag[:, c, :], bnst[:, :, :]).then_inc(S["gstat"], 1)
            dve.wait_ge(S["gstat"], c + 1)
            if c >= 1:
                z_lo(c - 1)
        z_lo(KC - 1)
        dve.wait_ge(S["bias_in"], 32)
        for t in range(NT):
            dve.wait_ge(S["w2_ps"], t + 1)
            dve.tensor_tensor(vb[:, t % 2, :], bank(t % 2), bias_row[:, 0, :], ALU.add).then_inc(S["h2b_tmp"], 1)
            dve.wait_ge(S["h2b_hi"], t + 1)
            dve.scalar_tensor_tensor(out=qh[:, t, 1, :], in0=vb[:, t % 2, :], scalar=dinv[:, t:t + 1],
                                     in1=qh[:, t, 0, :].bitcast(F32), op0=ALU.mult,
                                     op1=ALU.subtract).then_inc(S["h2b_lo"], 1)
        for t in range(NT):
            rest_of_counts(2 * KC + t, slice(t * P, (t + 1) * P))
            dve.wait_ge(S["agg2_ps"], t + 1)
            if t >= 2:
                dve.wait_ge(S[f"out_done{t % 2}"], 16 * (t // 2))
            dve.scalar_tensor_tensor(out=xt[:, t % 2, :], in0=bank(2 + t % 2), scalar=dinv[:, t:t + 1],
                                     in1=x1[:, t, :], op0=ALU.mult, op1=ALU.add).then_inc(S["out_ready"], 1)

    @block.tensor
    def _(pe):
        def three(out_, stat, mov, first, last):
            pe.matmul(out_, stat(1), mov(0), start=first, stop=False)
            pe.matmul(out_, stat(0), mov(1), start=False, stop=False)
            return pe.matmul(out_, stat(0), mov(0), start=False, stop=last)

        pe.wait_ge(S["consts"], 3)
        pe.wait_ge(S["edge_f_ready"], 1)
        for i in range(2):
            m = pe.transpose(bank(6)[:, i * P:(i + 1) * P], edge_f[:, i, :], ident[:, :])
        m.then_inc(S["ecol_ps"], 1)

        def hT_turn(t):
            pe.wait_ge(S["h_ready"], t + 1)
            if t >= 2:
                pe.wait_ge(S["hT_lo"], t - 1)
            for k in range(KC):
                m = pe.transpose(bank(4 + t % 2)[:, k * P:(k + 1) * P], ht[:, k * P:(k + 1) * P], ident[:, :])
            m.then_inc(S["hT_ps"], 1)

        def adj_turn(b):
            pe.wait_ge(S["adjT_ready"], b + 1)
            if b >= 2:
                pe.wait_ge(S["adj_evac"], b - 1)
            for s in range(NT):
                m = pe.transpose(bank(6 + b % 2).bitcast(BF16)[:, s * P:(s + 1) * P],
                                 adjT[:, b % 2, s * P:(s + 1) * P], identb[:, :])
            m.then_inc(S["adj_ps"], 1)

        pe.wait_ge(S["ecol_ready"], 1)
        pe.wait_ge(S["bounds_ready"], 1)
        pe.sem_inc(S["onehots_used"], RING)
        used = pe.alloc_register("used")
        pe.reg_mov(used, 0)
        for b in range(NT):
            if b >= 2:
                pe.wait_ge(S["c16"], b - 1)
            for n in range(2):
                pe.matmul(ps[:, 2 * (b % 2) + n, 0:32], zerob[:, :], zerob[:, 0:32], start=True, stop=False,
                          skip_group_check=True)
            first = pe.value_load(lohi[0:1, b:b + 1], min_val=0, max_val=NCH - 1)
            end = pe.value_load(lohi[0:1, NT + b:NT + b + 1], min_val=1, max_val=NCH)
            with pe.Fori(first, end) as c:
                k = pe.snap(used, min_val=0, max_val=NT * NCH)
                slot = k & (RING - 1)
                pe.wait_ge(S["onehots"], k + 1)
                for n in range(2):
                    m = pe.matmul(ps[:, 2 * (b % 2) + n, :],
                                  dst_oh[:, bass.ds(slot, 1), :].rearrange("p a n -> p (a n)"),
                                  src_oh[:, bass.ds(slot, 1), n * HALF:(n + 1) * HALF].rearrange("p a n -> p (a n)"),
                                  start=False, stop=False, skip_group_check=True)
                m.then_inc(S["onehots_used"], 1)
                pe.reg_add(used, used, 1)
            for n in range(2):
                m = pe.matmul(ps[:, 2 * (b % 2) + n, 0:32], zerob[:, :], zerob[:, 0:32], start=False, stop=True,
                              skip_group_check=True)
            m.then_inc(S["c_done"], 1)
            hT_turn(b)
            if b >= 1:
                adj_turn(b - 1)
        adj_turn(NT - 1)

        pe.wait_ge(S["adj_evac"], NT)
        pe.wait_ge(S["hT_lo"], NT)
        pe.wait_ge(S["c16"], NT)

        def kq_group(g, wpart, n, c):
            if g >= 4:
                pe.wait_ge(S["kq_lo"], g - 3)
            for k in range(KC):
                m = three(bank(4 + g % 4), lambda a: wpart[:, a, k, c * P:(c + 1) * P],
                          lambda a: hT[:, a, k, n * HALF:(n + 1) * HALF], k == 0, k == KC - 1)
            m.then_inc(S["q_ps"], 1)

        pe.wait_ge(S["stage_lo"], LOADS)
        for g in range(2 * KC):
            kq_group(g, wA, g // KC, g % KC)
        pe.wait_ge(S["stage_lo"], 2 * LOADS)
        for t in range(NT):
            if t >= 4:
                pe.wait_ge(S["v_tmp"], t - 3)
            for k in range(KC):
                m = three(bank(t % 4), lambda a: hT[:, a, k, t * P:(t + 1) * P], lambda a: wB[:, a, k, :],
                          k == 0, k == KC - 1)
            m.then_inc(S["v_ps"], 1)
        pe.wait_ge(S["stage_lo"], 3 * LOADS)
        for g in range(2 * KC):
            kq_group(2 * KC + g, wA, g // KC, g % KC)

        def scores(t):
            if t == 0:
                pe.wait_ge(S["kq_lo"], 3 * KC)
                pe.wait_ge(S["v_tmp"], NT)
            if t == 4:
                pe.wait_ge(S["kq_lo"], 4 * KC)
            if t >= 2:
                pe.wait_ge(S["masked"], t - 1)
            for n in range(2):
                for k in range(KC):
                    m = three(bank(2 * (t % 2) + n), lambda a: qh[:, t, a, k * P:(k + 1) * P],
                              lambda a: kT[:, a, k, n * HALF:(n + 1) * HALF], k == 0, k == KC - 1)
            m.then_inc(S["s_ps"], 1)

        def p_turn(t):
            pe.wait_ge(S["exp_done"], t + 1)
            if t == 0:
                pe.wait_ge(S["kq_lo"], 4 * KC)
            if t >= 1:
                pe.wait_ge(S["p_lo"], t)
            for k in range(NT):
                m = pe.transpose(ps[:, 4 + k // 4, (k % 4) * P:(k % 4 + 1) * P], T[:, t % 2, k * P:(k + 1) * P],
                                 ident[:, :])
            m.then_inc(S["pT_ps"], 1)

        def weighted_v(t):
            pe.wait_ge(S["p_lo"], t + 1)
            if t == 0:
                pe.wait_ge(S["v_lo"], NT)
            if t >= 1:
                pe.wait_ge(S["x1_ready"], t)
            for k in range(NT):
                m = three(bank(6), lambda a: pT[:, t % 2, a, k, :], lambda a: v[:, k, a, :], k == 0, k == NT - 1)
            m.then_inc(S["pv_ps"], 1)

        def h2_turn(t):
            pe.wait_ge(S["h2_ready"], t + 1)
            if t >= 1:
                pe.wait_ge(S["h1_tmp"], t)
            for k in range(KC):
                m = pe.transpose(bank(7)[:, k * P:(k + 1) * P], ht[:, k * P:(k + 1) * P], ident[:, :])
            m.then_inc(S["h2T_ps"], 1)

        def times_w1(t):
            pe.wait_ge(S["h2T_lo"], t + 1)
            if t == 0:
                pe.wait_ge(S["stage_lo"], 4 * LOADS)
            for k in range(KC):
                m = three(bank(7), lambda a: hnT[:, a, k * P:(k + 1) * P], lambda a: wB[:, a, k, :],
                          k == 0, k == KC - 1)
            m.then_inc(S["w1_ps"], 1)

        for i in range(NT + 2):
            if i < NT:
                scores(i)
            if i >= 2:
                h2_turn(i - 2)
            if 1 <= i <= NT:
                p_turn(i - 1)
            if i >= 2:
                times_w1(i - 2)
            if 1 <= i <= NT:
                weighted_v(i - 1)

        pe.wait_ge(S["diag_ready"], 1)
        for n in range(2):
            m = pe.matmul(bank(n), ones[:, :], T[:, 0, n * HALF:(n + 1) * HALF], start=True, stop=True)
        m.then_inc(S["bc_ps"], 1)
        pe.wait_ge(S["flag_ready"], 1)
        large = pe.value_load(flag[0:1, 0:1], min_val=0, max_val=1)
        pe.sem_inc(S["res_used"], 1)

        def rest_of_counts(g, product):
            with pe.If(large > 0):
                with pe.Fori(0, NT) as d:
                    pe.wait_ge(S["res_ready"], d + g * NT + 1)
                    product(1, d)
                    product(0, d).then_inc(S["res_used"], 1)

        pe.wait_ge(S["h1_lo"], NT)
        for g in range(2 * KC):
            c, n = divmod(g, 2)
            if g >= 4:
                pe.wait_ge(S["g_ready"], g - 3)
            for d in range(NT):
                if g == 0:
                    pe.wait_ge(S["cnt_ready"], d + 1)
                for a in (1, 0):
                    if d == NT - 1 and a == 0:
                        rest_of_counts(g, lambda a, d: pe.matmul(bank(g % 4 + 2), res_h[:, a, :], res[:, :],
                                                                 start=False, stop=False, skip_group_check=True))
                    m = pe.matmul(bank(g % 4 + 2), qh[:, d, a, c * P:(c + 1) * P],
                                  cnt[:, d, n * HALF:(n + 1) * HALF], start=(d == 0 and a == 1),
                                  stop=(d == NT - 1 and a == 0))
            m.then_inc(S["agg1_ps"], 1)
        pe.wait_ge(S["stage_lo"], 5 * LOADS)
        pe.wait_ge(S["z_lo"], KC)
        pe.wait_ge(S["bc_ready"], 1)
        for t in range(NT):
            if t >= 2:
                pe.wait_ge(S["h2b_tmp"], t - 1)
            for k in range(KC):
                m = three(bank(t % 2), lambda a: zT[:, a, k, t * P:(t + 1) * P], lambda a: w2[:, a, k, :],
                          k == 0, k == KC - 1)
            m.then_inc(S["w2_ps"], 1)
        for t in range(NT):
            if t >= 2:
                pe.wait_ge(S["out_ready"], t - 1)
            for d in range(NT):
                if t == 0:
                    pe.wait_ge(S["h2b_lo"], d + 1)
                for a in (1, 0):
                    if d == NT - 1 and a == 0:
                        rest_of_counts(2 * KC + t, lambda a, d: pe.matmul(
                            bank(2 + t % 2), res[:, 0:P],
                            qh[:, bass.ds(d, 1), a, :].rearrange("p t n -> p (t n)"),
                            start=False, stop=False, skip_group_check=True))
                    m = pe.matmul(bank(2 + t % 2), cnt[:, d, t * P:(t + 1) * P], qh[:, d, a, :],
                                  start=(d == 0 and a == 1), stop=(d == NT - 1 and a == 0))
            m.then_inc(S["agg2_ps"], 1)

    ctx.close()


_INS = ["x", "src", "dst", "L0_gnn_Wq", "L0_gnn_bq", "L0_gnn_Wk", "L0_gnn_bk", "L0_gnn_Wv", "L0_gnn_bv",
        "L1_gnn_W1", "L1_gnn_b1", "L1_gnn_gamma", "L1_gnn_beta", "L1_gnn_W2", "L1_gnn_b2"]


def kernel(**inputs):
    import numpy as np
    import concourse.bacc as bacc
    from concourse.bass_utils import run_bass_kernel_spmd

    nc = bacc.Bacc("TRN2", target_bir_lowering=False, num_devices=1, dynamic_dma_scratch_size=1024)
    arrays, args = {}, []
    for name in _INS:
        a = np.ascontiguousarray(inputs[name])
        arrays[name + "_in"] = a
        args.append(nc.dram_tensor(name + "_in", a.shape, mybir.dt.from_np(a.dtype), kind="ExternalInput").ap())
    args.append(nc.dram_tensor("out_0", (N, D), F32, kind="ExternalOutput").ap())
    gnn_kernel(nc, *args)
    r = run_bass_kernel_spmd(nc, [arrays], core_ids=[0])
    return r.results[0]["out_0"]
```

```python
from contextlib import ExitStack

import concourse.bass as bass
from concourse import mybir

P = 128
N = 1024
D = 512
E = 16384
NT = N // P
KC = D // P
NCH = E // P
HALF = 512
UNROLL = 4
RING = 4
BLOCKS = (7, 0, 1, 2, 3, 4, 5, 6)
QUOTAS = (3, 2, 2, 2, 2, 2, 2, 1)
TURNS = ((0, 1, 2, 3), (4, 5), (6, 7))
KV_BANKS = 3
LOADS = 2
XT = 4
EXACT = 4096.0
SCALE = float(D) ** -0.5
NEG = -1.0e6
EPS = 1e-5

ALU = mybir.AluOpType
ACT = mybir.ActivationFunctionType
AX = mybir.AxisListType
F32 = mybir.dt.float32
F32R = mybir.dt.float32r
BF16 = mybir.dt.bfloat16
F16 = mybir.dt.float16
I32 = mybir.dt.int32
I16 = mybir.dt.int16
U8 = mybir.dt.uint8


def gnn_kernel(nc, x, src, dst, Wq, bq, Wk, bk, Wv, bv, W1, b1, gamma, beta, W2, b2, out):
    ctx = ExitStack()

    def sb(name, shape, dt, where=ctx):
        return where.enter_context(nc.sbuf_tensor(name, shape, dt))

    def shared(*groups):
        made = []
        for g in groups:
            s = ExitStack()
            made += [sb(name, shape, dt, s) for name, shape, dt in g]
            s.close()
        return made

    def hold(name, kib):
        sb(name, [P, 256 * kib], F32)

    hT, pT, w2, pT_, w2_raw, g32 = shared(
        [("hT", [P, 2, KC, N], F32R)],
        [("pT", [P, 2, 2, NT, P], F32R), ("w2", [P, 2, KC, D], F32R)],
        [("pT_", [P, 2, 2, NT, P], F32R), ("w2_raw", [P, 2, KC, D], F32)],
        [("g32", [P, KC, N], F32)])
    hold("region_hT", 32)
    wA, wA_raw, x1 = shared([("wA", [P, 2, KC, D], F32R)],
                            [("wA_raw", [P, 2, KC, D], F32)],
                            [("x1", [P, NT, D], F32)])
    hold("region_wA", 16)
    wB, wB_raw = shared([("wB", [P, 2, KC, D], F32R)], [("wB_raw", [P, 2, KC, D], F32)])
    hold("region_wB", 16)
    qh, src_oh, edge_i, edge_f = shared(
        [("qh", [P, NT, 2, KC * P], F32R)],
        [("src_oh", [P, RING, UNROLL, N], BF16)],
        [("edge_i", [P, 2, P], I32), ("edge_f", [P, 2, P], F32)])
    hold("region_qh", 32)
    kT, cnt = shared([("kT", [P, 2, KC, N], F32R)], [("cnt", [P, NT, N], F32R)])
    hold("region_kT", 32)
    v, zT = shared([("v", [P, NT, 2, D], F32R)], [("zT", [P, 2, KC, N], F32R)])
    hold("region_v", 32)
    T = sb("T", [P, 2, N], F32)
    cnt16 = sb("cnt16", [P, NT, N], I16)
    adj = sb("adj", [P, NT, N], U8)
    xt = sb("xt", [P, XT, D], F32)
    ht, iota = shared([("ht", [P, D], F32)], [("iota", [P, N], F16)])
    hold("region_ht", 2)
    dst_oh = sb("dst_oh", [P, RING, UNROLL, P], BF16)
    ecol = sb("ecol", [P, 2, NCH], F32)
    hnT, res, res_h, adjT = shared([("hnT", [P, 2, KC * P], F32R)],
                             [("res", [P, HALF], F32R), ("res_h", [P, 2, P], F32R)],
                             [("adjT", [P, 2, N], BF16)])
    hold("region_hnT", 4)
    vb = sb("vb", [P, 2, D], F32)
    bias_row = sb("bias_row", [P, 2, D], F32)
    ident = sb("ident", [P, P], F32)
    identb = sb("identb", [P, P], BF16)
    zerob = sb("zerob", [P, P], BF16)
    ones = sb("ones", [P, P], F32)
    half_pow = sb("half_pow", [P, NT], F32)
    bcol = sb("bcol", [P, 4, KC], F32)
    lohi = sb("lohi", [1, 2 * NT], I32)
    blk0 = sb("blk0", [P, NT], F32)
    chunk1 = sb("chunk1", [P, 2], F32)
    ext = sb("ext", [P, 2], F32)
    hit = sb("hit", [P, 3, NT], F32)
    span = sb("span", [P, 2, NT], F32)
    spanr = sb("spanr", [P, 2, NT], F32)
    lim = sb("lim", [P, 2, NT], F32)
    lsum = sb("lsum", [P, 4, NT], F32)
    lnc = sb("lnc", [P, 6, NT], F32)
    deg = sb("deg", [P, NT], F32)
    dinv = sb("dinv", [P, NT], F32)
    degm = sb("degm", [P, 4], F32)
    flag = sb("flag", [1, 1], I32)
    smx = sb("smx", [P, 4, NT], F32)
    bnst = sb("bnst", [P, 2, 6], F32)
    bnag = sb("bnag", [P, NT, 2], F32)
    bnc = sb("bnc", [P, 4, KC], F32)
    lnb = sb("lnb", [P, 4, NT], F32)

    ps = ctx.enter_context(nc.psum_tensor("ps", [P, 8, HALF], F32))
    bank = lambda b: ps[:, b, :]

    sem_names = """ident_ready iota_ready consts item_raw item_biased item_hi item_lo cnt_act cnt_dve edges_in x_in0 x_in1 x_in2 x_in3 wA_in0 wA_in1 wB_in0 wB_in1 w2_in0 w2_in1 w_hi w_lo bcol_in bias_in b1_in
    edge_f_ready ecol_ps ecol_ready span_ready span_max bounds_ready onehots onehots_used c_done c16
    adjT_ready adj_ps adj_evac  dinv_ready ln_sum ln_mean ln_sq ln_coef h_ready hT_ps hT_hi hT_lo
    kv_ps q_ps q_hi q_lo s_ps mask_set masked top_ready exp_done rinv_ready pT_ps p_hi p_lo
    pv_ps x1_ready bn_ready ln2_coef h2_ready h2T_ps h2T_hi h2T_lo w1_ps h1_tmp h1_hi h1_lo
    diag_ready bc_ps bc_ready cnt_ready agg1_ps g_ready gstat z_coef z_ready z_hi z_lo w2_ps h2b_tmp h2b_hi h2b_lo
    agg2_ps out_ready out_done0 out_done1 out_done2 out_done3 small pool_small flag_max flag_ready res_ready res_used vb_small""".split()
    S = {n: ctx.enter_context(nc.semaphore(n)) for n in sem_names}

    kv = [("k", n, c) if what == "k" else ("v", KC * n + c, 0) for n in range(2) for what in "kv" for c in range(KC)]
    behind = [kv[sum(QUOTAS[:i]):sum(QUOTAS[:i + 1])] for i in range(NT)]
    kv_bank = lambda item: 5 + kv.index(item) % KV_BANKS
    EARLY = len(TURNS[0])
    items = []
    for i in range(NT):
        items += [("h", t, 0) for t in (TURNS[i] if 0 < i < len(TURNS) else ())] + behind[i]
    nth = lambda item: items.index(item) + 1
    turn_bank = lambda t: (2, 3, 5, 6)[t] if t < EARLY else 2 + t % 2
    q_bank = lambda g: 4 + g if g < KC else 6 + g % 2
    adj_bank = lambda i: 4 - i % 2

    def item_dest(item, part):
        what, n, c = item
        if what == "h":
            return hT[:, part, :, n * P:(n + 1) * P]
        return kT[:, part, c, n * HALF:(n + 1) * HALF] if what == "k" else v[:, n, part, :]

    weights = [(Wk, wA, wA_raw, "wA_in", 16), (Wv, wB, wB_raw, "wB_in", 16), (Wq, wA, wA_raw, "wA_in", 32),
               (W1, wB, wB_raw, "wB_in", 32), (W2, w2, w2_raw, "w2_in", 16)]
    def weight_load(i, j, what):
        k = KC // LOADS
        w, raw = weights[i][1:3]
        at, part = {"hi": (w, 0), "lo": (w, 1), "raw": (raw, 1)}[what]
        return at[:, part, j * k:(j + 1) * k, :]

    ACT_COUNTS, DVE_COUNTS = (0, 1, 2, 3), (4, 5, 6, 7)
    SPLIT_Q = next(i for i in range(NT) if kv[-KC - 1] in behind[i])

    block = ctx.enter_context(nc.Block())

    @block.sync
    def _(sp):
        sp.dma_start(edge_i[:, 0, :], dst.rearrange("(c j) -> c j", j=P)).then_inc(S["edges_in"], 16)
        sp.dma_start(edge_i[:, 1, :], src.rearrange("(c j) -> c j", j=P)).then_inc(S["edges_in"], 16)

        def load_x(n):
            if XT <= n < NT + XT:
                sp.wait_ge(S["h_ready"], n - XT + 1)
            if n >= NT + XT:
                sp.wait_ge(S["x1_ready"], n - NT - XT + 1)
            sp.dma_start(xt[:, n % XT, :], x[(n % NT) * P:(n % NT + 1) * P, :]).then_inc(S[f"x_in{n % XT}"], 16)

        def load_w(i):
            k = KC // LOADS
            for j in range(LOADS):
                sp.dma_start(weight_load(i, j, "raw"), weights[i][0].rearrange("(k p) n -> p k n", p=P)[
                    :, j * k:(j + 1) * k, :]).then_inc(S[f"{weights[i][3]}{j}"], 16)

        for t in range(XT):
            load_x(t)
        load_w(0)
        for i, b in enumerate((bq, bk, gamma, beta)):
            sp.dma_start(bcol[:, i, :], b.rearrange("(c p) -> p c", p=P),
                         allow_slow_non_contiguous=True).then_inc(S["bcol_in"], 16)
        load_w(1)
        sp.dma_start(bias_row[:, 0, :], bv.rearrange("(o n) -> o n", o=1).to_broadcast([P, D])).then_inc(S["bias_in"], 16)
        sp.dma_start(bias_row[:, 1, :], b1.rearrange("(o n) -> o n", o=1).to_broadcast([P, D])).then_inc(S["b1_in"], 16)
        for t in range(XT, NT):
            load_x(t)
        for t in range(XT):
            load_x(NT + t)
        sp.wait_ge(S["kv_ps"], kv.index(("k", 1, KC - 1)) + 1)
        load_w(2)
        sp.wait_ge(S["kv_ps"], len(kv))
        load_w(3)
        sp.wait_ge(S["item_biased"], NT)
        sp.dma_start(bias_row[:, 0, :], b2.rearrange("(o n) -> o n", o=1).to_broadcast([P, D])).then_inc(S["bias_in"], 16)
        sp.wait_ge(S["q_ps"], 2 * KC)
        load_w(4)
        for t in range(XT, NT):
            load_x(NT + t)
        for t in range(NT):
            sp.wait_ge(S["out_ready"], t + 1)
            sp.dma_start(out[t * P:(t + 1) * P, :], xt[:, t % XT, :]).then_inc(S[f"out_done{t % XT}"], 16)
        for u in range(XT):
            sp.wait_ge(S[f"out_done{u}"], 16 * NT // XT)

    @block.gpsimd
    def _(pool):
        def pw(out_, in_, w):
            return pool.tensor_tensor(out_, in_, half_pow[:, 0:w], ALU.pow)

        pool.memset(ident[:, :], 0.0).then_inc(S["small"], 1)
        pool.iota(blk0[:, :], pattern=[[P, NT]], base=0, channel_multiplier=0,
                  allow_small_or_imprecise_dtypes=True)
        pool.iota(chunk1[:, 0:1], pattern=[[0, 1]], base=1, channel_multiplier=1,
                  allow_small_or_imprecise_dtypes=True)
        pool.iota(chunk1[:, 1:2], pattern=[[0, 1]], base=NCH, channel_multiplier=-1,
                  allow_small_or_imprecise_dtypes=True).then_inc(S["iota_ready"], 1)
        pool.wait_ge(S["small"], 1)
        pool.affine_select(out=ident[:, :], in_=ident[:, :], compare_op=ALU.not_equal, fill=1.0, base=0,
                           pattern=[[-1, P]], channel_multiplier=1).then_inc(S["ident_ready"], 1)
        pool.iota(iota[:, :], pattern=[[1, N]], base=0, channel_multiplier=0,
                  allow_small_or_imprecise_dtypes=True).then_inc(S["iota_ready"], 1)
        pool.memset(zerob[:, :], 0.0)
        pool.memset(half_pow[:, :], -0.5).then_inc(S["consts"], 1)

        pool.wait_ge(S["span_ready"], 1)
        pool.partition_all_reduce(spanr[:, :, :].rearrange("p a b -> p (a b)"),
                                  span[:, :, :].rearrange("p a b -> p (a b)"), P,
                                  bass.bass_isa.ReduceOp.max).then_inc(S["span_max"], 1)
        pool.wait_ge(S["ident_ready"], 1)
        pool.tensor_copy(identb[:, :], ident[:, :])
        pool.memset(ones[:, :], 1.0).then_inc(S["consts"], 1)

        n_small = [0]

        def step(ins):
            n_small[0] += 1
            ins.then_inc(S["pool_small"], 1)
            pool.wait_ge(S["pool_small"], n_small[0])

        def ln1_mean(t):
            pool.wait_ge(S["ln_sum"], t + 1)
            pool.tensor_scalar(lnc[:, 0, t:t + 1], lsum[:, 0, t:t + 1], -1.0 / D, 0.0, ALU.mult,
                               ALU.add).then_inc(S["ln_mean"], 1)

        def ln1_coef(t):
            pool.wait_ge(S["ln_sq"], t + 1)
            step(pool.tensor_scalar(lnc[:, 1, t:t + 1], lsum[:, 1, t:t + 1], 1.0 / D, EPS, ALU.mult, ALU.add))
            step(pw(lnc[:, 2, t:t + 1], lnc[:, 1, t:t + 1], 1))
            pool.tensor_tensor(lnc[:, 3, t:t + 1], lnc[:, 0, t:t + 1], lnc[:, 2, t:t + 1],
                               ALU.mult).then_inc(S["ln_coef"], 1)

        def split_w(i):
            for j in range(LOADS):
                pool.wait_ge(S["w_hi"], i * LOADS + j + 1)
                pool.tensor_tensor(weight_load(i, j, "lo"), weight_load(i, j, "raw"), weight_load(i, j, "hi").bitcast(F32),
                                   ALU.subtract).then_inc(S["w_lo"], 1)

        def split_item(item):
            i = nth(item)
            buf = vb[:, i % 2, :]
            if item[0] == "v":
                pool.wait_ge(S["item_raw"], i)
                pool.tensor_tensor(buf, buf, bias_row[:, 0, :], ALU.add).then_inc(S["item_biased"], 1)
            pool.wait_ge(S["item_hi"], i)
            if item[0] == "h":
                buf = buf.rearrange("p (k n) -> p k n", k=KC)
            pool.tensor_tensor(item_dest(item, 1), buf, item_dest(item, 0).bitcast(F32),
                               ALU.subtract).then_inc(S["item_lo"], 1)

        for t in TURNS[0]:
            ln1_mean(t)
            ln1_coef(t)
        split_w(0)
        split_w(1)
        pool.wait_ge(S["bias_in"], 16)
        for i in range(NT):
            if 0 < i < len(TURNS):
                for t in TURNS[i]:
                    split_item(("h", t, 0))
            if i + 1 < len(TURNS):
                for t in TURNS[i + 1]:
                    ln1_mean(t)
                    ln1_coef(t)
            for item in behind[i]:
                split_item(item)
            if i == SPLIT_Q:
                split_w(2)
        pool.wait_ge(S["flag_max"], 1)
        pw(dinv[:, :], deg[:, :], NT).then_inc(S["dinv_ready"], 1)
        pool.partition_all_reduce(degm[:, 2:3], degm[:, 1:2], P,
                                  bass.bass_isa.ReduceOp.max).then_inc(S["flag_max"], 1)

        def mask_fill(t):
            if t >= 2:
                pool.wait_ge(S["pT_ps"], t - 1)
            pool.memset(T[:, t % 2, :], NEG / SCALE).then_inc(S["mask_set"], 1)

        def ln2_coef(t):
            pool.wait_ge(S["bn_ready"], t + 1)
            step(pool.tensor_scalar(lnb[:, 0, t:t + 1], bnag[:, t, 1:2], 1.0, EPS, ALU.mult, ALU.add))
            step(pw(lnb[:, 1, t:t + 1], lnb[:, 0, t:t + 1], 1))
            step(pool.tensor_scalar(lnb[:, 2, t:t + 1], bnag[:, t, 0:1], -1.0, 0.0, ALU.mult, ALU.add))
            pool.tensor_tensor(lnb[:, 3, t:t + 1], lnb[:, 2, t:t + 1], lnb[:, 1, t:t + 1],
                               ALU.mult).then_inc(S["ln2_coef"], 1)

        mask_fill(0)
        mask_fill(1)
        split_w(3)
        for t in range(NT):
            ln2_coef(t)
            if t + 2 < NT:
                mask_fill(t + 2)
            if t == 1:
                split_w(4)
        for c in range(KC):
            pool.wait_ge(S["gstat"], c + 1)
            step(pool.tensor_scalar(bnc[:, 0, c:c + 1], bnag[:, c, 1:2], 1.0, EPS, ALU.mult, ALU.add))
            step(pw(bnc[:, 1, c:c + 1], bnc[:, 0, c:c + 1], 1))
            if c == 0:
                pool.wait_ge(S["bcol_in"], 64)
            step(pool.tensor_tensor(bnc[:, 2, c:c + 1], bnc[:, 1, c:c + 1], bcol[:, 2, c:c + 1], ALU.mult))
            step(pool.tensor_tensor(bnc[:, 0, c:c + 1], bnag[:, c, 0:1], bnc[:, 2, c:c + 1], ALU.mult))
            pool.tensor_tensor(bnc[:, 3, c:c + 1], bcol[:, 3, c:c + 1], bnc[:, 0, c:c + 1],
                               ALU.subtract).then_inc(S["z_coef"], 1)

    @block.scalar
    def _(act):
        def split_w(i):
            for j in range(LOADS):
                act.wait_ge(S[f"{weights[i][3]}{j}"], weights[i][4])
                act.activation(weight_load(i, j, "hi"), weight_load(i, j, "raw"),
                               ACT.Copy).then_inc(S["w_hi"], 1)

        def hT_hi(t):
            act.wait_ge(S["hT_ps"], t + 1)
            act.activation(hT[:, 0, :, t * P:(t + 1) * P], bank(turn_bank(t)).rearrange("p (k n) -> p k n", k=KC),
                           ACT.Copy).then_inc(S["hT_hi"], 1)

        def adj_out(i):
            act.wait_ge(S["adj_ps"], i + 1)
            act.activation(adj[:, :, BLOCKS[i] * P:(BLOCKS[i] + 1) * P],
                           bank(adj_bank(i)).bitcast(BF16).rearrange("p (s n) -> p s n", s=NT),
                           ACT.Copy).then_inc(S["adj_evac"], 1)

        def layer_norm(t):
            h = T[:, (t % KC) // 2, (t % 2) * D:(t % 2 + 1) * D]
            act.wait_ge(S[f"x_in{t % XT}"], 16 * (t // XT + 1))
            if t >= KC:
                act.wait_ge(S["hT_ps"], t - KC + 1)
            act.activation(h, xt[:, t % XT, :], ACT.Copy, accum_out=lsum[:, 0, t:t + 1]).then_inc(S["ln_sum"], 1)
            act.wait_ge(S["ln_mean"], t + 1)
            act.activation(h, xt[:, t % XT, :], ACT.Square, bias=lnc[:, 0, t:t + 1],
                           accum_out=lsum[:, 1, t:t + 1]).then_inc(S["ln_sq"], 1)
            act.wait_ge(S["ln_coef"], t + 1)
            act.activation(h, xt[:, t % XT, :], ACT.Relu, bias=lnc[:, 3, t:t + 1],
                           scale=lnc[:, 2, t:t + 1]).then_inc(S["h_ready"], 1)

        def counts(i):
            b = BLOCKS[i]
            act.wait_ge(S["c_done"], i + 1)
            act.activation(cnt16[:, b, :], ps[:, 0:2, :].rearrange("p a n -> p (a n)"), ACT.Copy,
                           accum_out=deg[:, b:b + 1]).then_inc(S["c16"], 1)

        def hi_of(item):
            i = nth(item)
            act.wait_ge(*((S["item_biased"], item[1] + 1) if item[0] == "v" else (S["item_raw"], i)))
            buf = vb[:, i % 2, :]
            if item[0] == "h":
                buf = buf.rearrange("p (k n) -> p k n", k=KC)
            act.activation(item_dest(item, 0), buf, ACT.Copy).then_inc(S["item_hi"], 1)

        late = []

        def take(item):
            what, n, c = item
            i = nth(item)
            act.wait_ge(S["hT_ps"], n + 1) if what == "h" else act.wait_ge(S["kv_ps"], kv.index(item) + 1)
            if i > 2:
                act.wait_ge(S["item_lo"], i - 2)
            if what == "k":
                ins = act.activation(vb[:, i % 2, :], bank(kv_bank(item)), ACT.Identity, bias=bcol[:, 1, c:c + 1])
            else:
                ins = act.activation(vb[:, i % 2, :], bank(turn_bank(n) if what == "h" else kv_bank(item)), ACT.Copy)
            ins.then_inc(S["item_raw"], 1)
            while late:
                hi_of(late.pop())
            if what == "v":
                late.append(item)
            else:
                hi_of(item)

        for t in TURNS[0]:
            layer_norm(t)
        split_w(0)
        act.wait_ge(S["bcol_in"], 64)
        for i in range(NT):
            if i < len(TURNS):
                for t in TURNS[i]:
                    hT_hi(t) if t < EARLY else take(("h", t, 0))
            counts(i)
            if i == 0:
                split_w(1)
            if i + 1 < len(TURNS):
                for t in TURNS[i + 1]:
                    layer_norm(t)
            if i >= 2:
                adj_out(i - 2)
            for item in behind[i]:
                take(item)
            while late:
                hi_of(late.pop())
            if i == SPLIT_Q:
                split_w(2)
        adj_out(NT - 2)
        adj_out(NT - 1)
        def q_hi(g):
            n, c = divmod(g, KC)
            act.wait_ge(S["q_ps"], g + 1)
            act.activation(qh[:, 4 * n:4 * n + 4, 0, c * P:(c + 1) * P], bank(q_bank(g)), ACT.Identity,
                           bias=bcol[:, 0, c:c + 1]).then_inc(S["q_hi"], 1)

        for g in range(KC):
            q_hi(g)

        def softmax_exp(t):
            act.wait_ge(S["top_ready"], t + 1)
            act.activation(T[:, t % 2, :], T[:, t % 2, :], ACT.Exp, bias=smx[:, 1, t:t + 1], scale=SCALE,
                           accum_out=smx[:, 2, t:t + 1]).then_inc(S["exp_done"], 1)

        def p_hi(t):
            act.wait_ge(S["pT_ps"], t + 1)
            if t >= 2:
                act.wait_ge(S["pv_ps"], t - 1)
            act.activation(pT[:, t % 2, 0, :, :], ps[:, 4:6, :].rearrange("p a (k n) -> p (a k) n", n=P),
                           ACT.Copy).then_inc(S["p_hi"], 1)

        def h2_relu(t):
            act.wait_ge(S["ln2_coef"], t + 1)
            if t >= 1:
                act.wait_ge(S["h2T_ps"], t)
            act.activation(ht[:, :], x1[:, t, :], ACT.Relu, bias=lnb[:, 3, t:t + 1],
                           scale=lnb[:, 1, t:t + 1]).then_inc(S["h2_ready"], 1)

        def h2T_hi(t):
            act.wait_ge(S["h2T_ps"], t + 1)
            if t >= 1:
                act.wait_ge(S["w1_ps"], t)
            act.activation(hnT[:, 0, :], bank(7), ACT.Copy).then_inc(S["h2T_hi"], 1)

        def h1_hi(t):
            act.wait_ge(S["h1_tmp"], t + 1)
            act.activation(qh[:, t, 0, :], vb[:, t % 2, :], ACT.Copy, scale=dinv[:, t:t + 1]).then_inc(S["h1_hi"], 1)

        def count_parts(blocks):
            for b in blocks:
                act.activation(cnt[:, b, :], cnt16[:, b, :], ACT.Copy).then_inc(S["cnt_act"], 1)

        act.wait_ge(S["dinv_ready"], 1)
        for i in range(NT + 2):
            if i >= 2:
                h2_relu(i - 2)
                h2T_hi(i - 2)
            if i == 1:
                q_hi(KC + 2)
                q_hi(KC + 3)
            if 1 <= i <= NT:
                p_hi(i - 1)
            if i == 0:
                q_hi(KC)
                q_hi(KC + 1)
            if i < NT:
                softmax_exp(i)
            if i == 0:
                split_w(3)
            if i == 3:
                split_w(4)
            if i >= 2:
                h1_hi(i - 2)
            if i == NT - 1:
                act.wait_ge(S["s_ps"], NT)
                count_parts(ACT_COUNTS)
        act.wait_ge(S["bc_ps"], 1)
        act.activation(T[:, 1, :], ps[:, 4:6, :].rearrange("p a n -> p (a n)"), ACT.Copy).then_inc(S["bc_ready"], 1)
        for c in range(KC):
            act.wait_ge(S["z_coef"], c + 1)
            act.activation(g32[:, c, :], g32[:, c, :], ACT.Relu, bias=bnc[:, 3, c:c + 1],
                           scale=bnc[:, 2, c:c + 1]).then_inc(S["z_ready"], 1)
            act.wait_ge(S["z_ready"], c + 1)
            act.activation(zT[:, 0, c, :], g32[:, c, :], ACT.Copy).then_inc(S["z_hi"], 1)
        for t in range(NT):
            act.wait_ge(S["h2b_tmp"], t + 1)
            act.activation(qh[:, t, 0, :], vb[:, t % 2, :], ACT.Copy, scale=dinv[:, t:t + 1]).then_inc(S["h2b_hi"], 1)

    @block.vector
    def _(dve):
        n_small = [0]

        def step(ins):
            n_small[0] += 1
            ins.then_inc(S["vb_small"], 1)
            dve.wait_ge(S["vb_small"], n_small[0])

        dve.wait_ge(S["edges_in"], 32)
        dve.tensor_copy(edge_f[:, :, :], edge_i[:, :, :]).then_inc(S["edge_f_ready"], 1)
        dve.wait_ge(S["edge_f_ready"], 1)
        dve.tensor_reduce(ext[:, 0:1], edge_f[:, 0, :], AX.X, ALU.min)
        step(dve.tensor_reduce(ext[:, 1:2], edge_f[:, 0, :], AX.X, ALU.max))
        dve.wait_ge(S["iota_ready"], 1)
        dve.tensor_scalar(hit[:, 0, :], blk0[:, :], ext[:, 1:2], None, ALU.is_le)
        step(dve.tensor_scalar(hit[:, 1, :], blk0[:, :], float(P - 1), ext[:, 0:1], ALU.add, ALU.is_ge))
        step(dve.tensor_tensor(hit[:, 2, :], hit[:, 0, :], hit[:, 1, :], ALU.mult))
        dve.tensor_scalar(span[:, 0, :], hit[:, 2, :], chunk1[:, 0:1], None, ALU.mult)
        dve.tensor_scalar(span[:, 1, :], hit[:, 2, :], chunk1[:, 1:2], None, ALU.mult).then_inc(S["span_ready"], 1)
        dve.wait_ge(S["ecol_ps"], 1)
        dve.tensor_copy(ecol[:, :, :], bank(6)[:, 0:2 * P].rearrange("p (a n) -> p a n", a=2)).then_inc(S["ecol_ready"], 1)
        dve.wait_ge(S["span_max"], 1)
        step(dve.tensor_scalar(lim[0:1, 0, :], spanr[0:1, 1, :], -1.0, float(NCH), ALU.mult, ALU.add))
        step(dve.tensor_scalar(lim[0:1, 0, :], lim[0:1, 0, :], float(NCH - 1), None, ALU.min))
        step(dve.scalar_tensor_tensor(out=lim[0:1, 1, :], in0=lim[0:1, 0, :], scalar=1.0, in1=spanr[0:1, 0, :],
                                      op0=ALU.add, op1=ALU.max))
        dve.tensor_copy(lohi[0:1, :], lim[0:1, :, :].rearrange("p a b -> p (a b)")).then_inc(S["bounds_ready"], 1)
        dve.wait_ge(S["bounds_ready"], 1)
        dve.wait_ge(S["ecol_ready"], 1)

        def adj_cols(i):
            b = BLOCKS[i]
            dve.wait_ge(S["c16"], i + 1)
            if i >= 2:
                dve.wait_ge(S["adj_ps"], i - 1)
            dve.tensor_scalar(adjT[:, i % 2, :], cnt16[:, b, :], 1.0, None, ALU.min).then_inc(S["adjT_ready"], 1)
            dve.wait_ge(S["adjT_ready"], i + 1)
            dve.tensor_tensor(cnt16[:, b, b * P:(b + 1) * P], cnt16[:, b, b * P:(b + 1) * P], identb[:, :], ALU.add)

        def hT_lo(t):
            dve.wait_ge(S["hT_hi"], t + 1)
            dve.tensor_tensor(hT[:, 1, :, t * P:(t + 1) * P],
                              bank(turn_bank(t)).rearrange("p (k n) -> p k n", k=KC),
                              hT[:, 0, :, t * P:(t + 1) * P].bitcast(F32), ALU.subtract).then_inc(S["hT_lo"], 1)

        made = dve.alloc_register("made")
        dve.reg_mov(made, 0)
        dve.wait_ge(S["iota_ready"], 2)
        dve.wait_ge(S["consts"], 2)
        for i, b in enumerate(BLOCKS):
            if i >= 2:
                adj_cols(i - 2)
            first = dve.value_load(lohi[0:1, b:b + 1], min_val=0, max_val=NCH - 1)
            end = dve.value_load(lohi[0:1, NT + b:NT + b + 1], min_val=1, max_val=NCH)
            with dve.Fori(first // UNROLL, (end + UNROLL - 1) // UNROLL) as c:
                k = dve.snap(made, min_val=0, max_val=NT * NCH // UNROLL)
                slot = k & (RING - 1)
                dve.wait_ge(S["onehots_used"], k + 1)
                for j in range(UNROLL):
                    dve.tensor_scalar(src_oh[:, bass.ds(slot, 1), j, :].rearrange("p a n -> p (a n)"), iota[:, :],
                                      ecol[:, 1, bass.ds(c * UNROLL + j, 1)], None, ALU.is_equal)
                last = dve.tensor_tensor(
                    dst_oh[:, bass.ds(slot, 1), :, :].rearrange("p a j n -> p (a j) n"),
                    iota[:, b * P:(b + 1) * P].rearrange("p (o n) -> p o n", o=1).to_broadcast([P, UNROLL, P]),
                    ecol[:, 0, bass.ds(c * UNROLL, UNROLL)].rearrange("p (n o) -> p n o", o=1).to_broadcast(
                        [P, UNROLL, P]), ALU.is_equal)
                last.then_inc(S["onehots"], 1)
                dve.reg_add(made, made, 1)
            if i == 0:
                for t in TURNS[0]:
                    hT_lo(t)
        adj_cols(NT - 2)
        adj_cols(NT - 1)
        step(dve.tensor_scalar(deg[:, :], deg[:, :], 1.0, None, ALU.add))
        dve.tensor_reduce(degm[:, 1:2], deg[:, :], AX.X, ALU.max).then_inc(S["flag_max"], 1)
        dve.wait_ge(S["flag_max"], 1)
        dve.wait_ge(S["flag_max"], 2)
        step(dve.tensor_scalar(degm[0:1, 3:4], degm[0:1, 2:3], EXACT, None, ALU.is_gt))
        dve.tensor_copy(flag[0:1, 0:1], degm[0:1, 3:4]).then_inc(S["flag_ready"], 1)

        def q_lo(g):
            n, c = divmod(g, KC)
            at = lambda part: qh[:, 4 * n:4 * n + 4, part, c * P:(c + 1) * P]
            dve.wait_ge(S["q_hi"], g + 1)
            dve.scalar_tensor_tensor(out=at(1), in0=bank(q_bank(g)).rearrange("p (t n) -> p t n", t=4),
                                     scalar=bcol[:, 0, c:c + 1], in1=at(0).bitcast(F32), op0=ALU.add,
                                     op1=ALU.subtract).then_inc(S["q_lo"], 1)

        dve.wait_ge(S["bcol_in"], 64)
        for g in range(KC):
            q_lo(g)

        def mask_and_max(t):
            dve.wait_ge(S["mask_set"], t + 1)
            dve.wait_ge(S["s_ps"], t + 1)
            dve.copy_predicated(T[:, t % 2, :], adj[:, t, :],
                                ps[:, 2 * (t % 2):2 * (t % 2) + 2, :].rearrange("p a n -> p (a n)")
                                ).then_inc(S["masked"], 1)
            dve.wait_ge(S["masked"], t + 1)
            step(dve.tensor_reduce(smx[:, 0, t:t + 1], T[:, t % 2, :], AX.X, ALU.max))
            dve.tensor_scalar(smx[:, 1, t:t + 1], smx[:, 0, t:t + 1], -SCALE, None, ALU.mult).then_inc(S["top_ready"], 1)

        def p_lo(t):
            dve.wait_ge(S["p_hi"], t + 1)
            dve.tensor_tensor(pT[:, t % 2, 1, :, :], ps[:, 4:6, :].rearrange("p a (k n) -> p (a k) n", n=P),
                              pT[:, t % 2, 0, :, :].bitcast(F32), ALU.subtract).then_inc(S["p_lo"], 1)
            dve.wait_ge(S["exp_done"], t + 1)
            dve.reciprocal(smx[:, 3, t:t + 1], smx[:, 2, t:t + 1]).then_inc(S["rinv_ready"], 1)

        def residual(t):
            n = NT + t
            dve.wait_ge(S[f"x_in{n % XT}"], 16 * (n // XT + 1))
            dve.wait_ge(S["rinv_ready"], t + 1)
            dve.wait_ge(S["pv_ps"], t + 1)
            dve.scalar_tensor_tensor(out=x1[:, t, :], in0=bank(6), scalar=smx[:, 3, t:t + 1], in1=xt[:, n % XT, :],
                                     op0=ALU.mult, op1=ALU.add).then_inc(S["x1_ready"], 1)
            dve.wait_ge(S["x1_ready"], t + 1)
            step(dve.bn_stats(bnst[:, 0, :], x1[:, t, :]))
            dve.bn_aggr(bnag[:, t, :], bnst[:, 0:1, :]).then_inc(S["bn_ready"], 1)
            dve.wait_ge(S["bn_ready"], t + 1)

        def h2T_lo(t):
            dve.wait_ge(S["h2T_hi"], t + 1)
            dve.tensor_tensor(hnT[:, 1, :], bank(7), hnT[:, 0, :].bitcast(F32), ALU.subtract).then_inc(S["h2T_lo"], 1)

        def h1_out(t):
            dve.wait_ge(S["w1_ps"], t + 1)
            dve.tensor_tensor(vb[:, t % 2, :], bank(7), bias_row[:, 1, :], ALU.add).then_inc(S["h1_tmp"], 1)
            dve.wait_ge(S["h1_hi"], t + 1)
            dve.scalar_tensor_tensor(out=qh[:, t, 1, :], in0=vb[:, t % 2, :], scalar=dinv[:, t:t + 1],
                                     in1=qh[:, t, 0, :].bitcast(F32), op0=ALU.mult,
                                     op1=ALU.subtract).then_inc(S["h1_lo"], 1)

        dve.wait_ge(S["b1_in"], 16)
        for i in range(NT + 2):
            if i >= 2:
                h2T_lo(i - 2)
            if i == 1:
                q_lo(KC + 2)
                q_lo(KC + 3)
            if 1 <= i <= NT:
                p_lo(i - 1)
            if i == 0:
                q_lo(KC)
                q_lo(KC + 1)
            if i < NT:
                mask_and_max(i)
            if i >= 2:
                h1_out(i - 2)
            if i == NT - 1:
                for b in DVE_COUNTS:
                    dve.tensor_copy(cnt[:, b, :], cnt16[:, b, :]).then_inc(S["cnt_dve"], 1)
                dve.wait_ge(S["pT_ps"], NT - 1)
                for b in range(NT):
                    ins = dve.tensor_scalar(T[:, 0, b * P:(b + 1) * P], ident[:, :], dinv[:, b:b + 1], None, ALU.mult)
                ins.then_inc(S["diag_ready"], 1)
            if 1 <= i <= NT:
                residual(i - 1)
        def z_lo(c):
            dve.wait_ge(S["z_hi"], c + 1)
            dve.tensor_tensor(zT[:, 1, c, :], g32[:, c, :], zT[:, 0, c, :].bitcast(F32),
                              ALU.subtract).then_inc(S["z_lo"], 1)

        dve.wait_ge(S["flag_ready"], 1)
        large = dve.value_load(flag[0:1, 0:1], min_val=0, max_val=1)

        def rest_of_counts(g, cols, h_cols=None):
            with dve.If(large > 0):
                with dve.Fori(0, NT) as d:
                    dve.wait_ge(S["res_used"], d + g * NT + 1)
                    w = cols.stop - cols.start
                    if h_cols:
                        dve.tensor_copy(res_h[:, :, :], qh[:, bass.ds(d, 1), :, h_cols].rearrange(
                            "p t a n -> p (t a) n").bitcast(F32))
                    dve.tensor_tensor(res[:, 0:w], cnt16[:, bass.ds(d, 1), cols].rearrange("p t n -> p (t n)"),
                                      cnt[:, bass.ds(d, 1), cols].rearrange("p t n -> p (t n)").bitcast(F32),
                                      ALU.subtract).then_inc(S["res_ready"], 1)

        dve.wait_ge(S["cnt_act"], len(ACT_COUNTS))
        dve.wait_ge(S["bc_ready"], 1)
        for c in range(KC):
            for n in range(2):
                g = 2 * c + n
                rest_of_counts(g, slice(n * HALF, (n + 1) * HALF), slice(c * P, (c + 1) * P))
                dve.wait_ge(S["agg1_ps"], g + 1)
                dve.tensor_tensor(g32[:, c, n * HALF:(n + 1) * HALF], bank(g),
                                  T[:, 1, n * HALF:(n + 1) * HALF], ALU.mult).then_inc(S["g_ready"], 1)
                dve.wait_ge(S["g_ready"], g + 1)
                step(dve.bn_stats(bnst[:, n, :], g32[:, c, n * HALF:(n + 1) * HALF]))
            dve.bn_aggr(bnag[:, c, :], bnst[:, :, :]).then_inc(S["gstat"], 1)
            dve.wait_ge(S["gstat"], c + 1)
            if c >= 1:
                z_lo(c - 1)
        z_lo(KC - 1)
        dve.wait_ge(S["bias_in"], 32)
        for t in range(NT):
            dve.wait_ge(S["w2_ps"], t + 1)
            dve.tensor_tensor(vb[:, t % 2, :], bank(t), bias_row[:, 0, :], ALU.add).then_inc(S["h2b_tmp"], 1)
            dve.wait_ge(S["h2b_hi"], t + 1)
            dve.scalar_tensor_tensor(out=qh[:, t, 1, :], in0=vb[:, t % 2, :], scalar=dinv[:, t:t + 1],
                                     in1=qh[:, t, 0, :].bitcast(F32), op0=ALU.mult,
                                     op1=ALU.subtract).then_inc(S["h2b_lo"], 1)
        for t in range(NT):
            rest_of_counts(2 * KC + t, slice(t * P, (t + 1) * P))
            dve.wait_ge(S["agg2_ps"], t + 1)
            if t >= XT:
                dve.wait_ge(S[f"out_done{t % XT}"], 16 * (t // XT))
            dve.scalar_tensor_tensor(out=xt[:, t % XT, :], in0=bank(t), scalar=dinv[:, t:t + 1],
                                     in1=x1[:, t, :], op0=ALU.mult, op1=ALU.add).then_inc(S["out_ready"], 1)

    @block.tensor
    def _(pe):
        def three(out_, stat, mov, first, last):
            pe.matmul(out_, stat(1), mov(0), start=first, stop=False)
            pe.matmul(out_, stat(0), mov(1), start=False, stop=False)
            return pe.matmul(out_, stat(0), mov(0), start=False, stop=last)

        pe.wait_ge(S["ident_ready"], 1)
        pe.wait_ge(S["edge_f_ready"], 1)
        for i in range(2):
            m = pe.transpose(bank(6)[:, i * P:(i + 1) * P], edge_f[:, i, :], ident[:, :])
        m.then_inc(S["ecol_ps"], 1)

        def hT_turn(t):
            pe.wait_ge(S["h_ready"], t + 1)
            if t == EARLY:
                pe.wait_ge(S["hT_lo"], EARLY)
            if t >= EARLY + 2:
                pe.wait_ge(S["item_raw"], nth(("h", t - 2, 0)))
            for k in range(KC):
                m = pe.transpose(bank(turn_bank(t))[:, k * P:(k + 1) * P],
                                 T[:, (t % KC) // 2, (t % 2) * D + k * P:(t % 2) * D + (k + 1) * P], ident[:, :])
            m.then_inc(S["hT_ps"], 1)

        def adj_turn(i):
            pe.wait_ge(S["adjT_ready"], i + 1)
            if i == 1:
                pe.wait_ge(S["item_raw"], nth(("h", NT - 1, 0)))
            if i >= 2:
                pe.wait_ge(S["adj_evac"], i - 1)
            for s in range(NT):
                m = pe.transpose(bank(adj_bank(i)).bitcast(BF16)[:, s * P:(s + 1) * P],
                                 adjT[:, i % 2, s * P:(s + 1) * P], identb[:, :])
            m.then_inc(S["adj_ps"], 1)

        pe.wait_ge(S["ecol_ready"], 1)
        pe.wait_ge(S["bounds_ready"], 1)
        pe.wait_ge(S["consts"], 2)
        pe.sem_inc(S["onehots_used"], RING)
        used = pe.alloc_register("used")
        pe.reg_mov(used, 0)
        def kv_product(item):
            what, n, c = item
            g = kv.index(item)
            if g == 0:
                pe.wait_ge(S["hT_lo"], EARLY)
                pe.wait_ge(S["w_lo"], LOADS)
            if item == ("v", 0, 0):
                pe.wait_ge(S["w_lo"], 2 * LOADS)
            if item == ("k", 1, 0):
                pe.wait_ge(S["item_lo"], nth(("h", NT - 1, 0)))
            if g >= KV_BANKS:
                pe.wait_ge(S["item_raw"], nth(kv[g - KV_BANKS]))
            for k in range(KC):
                if what == "k":
                    m = three(bank(kv_bank(item)), lambda a: wA[:, a, k, c * P:(c + 1) * P],
                              lambda a: hT[:, a, k, n * HALF:(n + 1) * HALF], k == 0, k == KC - 1)
                else:
                    m = three(bank(kv_bank(item)), lambda a: hT[:, a, k, n * P:(n + 1) * P],
                              lambda a: wB[:, a, k, :], k == 0, k == KC - 1)
            m.then_inc(S["kv_ps"], 1)

        for i, b in enumerate(BLOCKS):
            if i >= 1:
                pe.wait_ge(S["c16"], i)
            for n in range(2):
                pe.matmul(ps[:, n, 0:32], zerob[:, :], zerob[:, 0:32], start=True, stop=False,
                          skip_group_check=True)
            first = pe.value_load(lohi[0:1, b:b + 1], min_val=0, max_val=NCH - 1)
            end = pe.value_load(lohi[0:1, NT + b:NT + b + 1], min_val=1, max_val=NCH)
            with pe.Fori(first // UNROLL, (end + UNROLL - 1) // UNROLL) as c:
                k = pe.snap(used, min_val=0, max_val=NT * NCH // UNROLL)
                slot = k & (RING - 1)
                pe.wait_ge(S["onehots"], k + 1)
                for j in range(UNROLL):
                    for n in range(2):
                        m = pe.matmul(ps[:, n, :], dst_oh[:, bass.ds(slot, 1), j, :].rearrange("p a n -> p (a n)"),
                                      src_oh[:, bass.ds(slot, 1), j, n * HALF:(n + 1) * HALF].rearrange(
                                          "p a n -> p (a n)"), start=False, stop=False, skip_group_check=True)
                m.then_inc(S["onehots_used"], 1)
                pe.reg_add(used, used, 1)
            for n in range(2):
                m = pe.matmul(ps[:, n, 0:32], zerob[:, :], zerob[:, 0:32], start=False, stop=True,
                              skip_group_check=True)
            m.then_inc(S["c_done"], 1)
            for t in TURNS[i] if i < len(TURNS) else ():
                hT_turn(t)
            if i >= 2:
                adj_turn(i - 2)
            for item in behind[i]:
                kv_product(item)
        adj_turn(NT - 2)
        adj_turn(NT - 1)

        def q_product(g):
            n, c = divmod(g, KC)
            if g == 0:
                pe.wait_ge(S["w_lo"], 3 * LOADS)
                pe.wait_ge(S["adj_evac"], NT - 1)
                pe.wait_ge(S["item_raw"], len(items))
            if g >= KC:
                pe.wait_ge(S["q_lo"], {0: 3, 1: 4, 2: 5, 3: 6}[g - KC])
            for k in range(KC):
                m = three(bank(q_bank(g)), lambda a: wA[:, a, k, c * P:(c + 1) * P],
                          lambda a: hT[:, a, k, n * HALF:(n + 1) * HALF], k == 0, k == KC - 1)
            m.then_inc(S["q_ps"], 1)

        for g in range(KC):
            q_product(g)

        def scores(t):
            if t == 0:
                pe.wait_ge(S["q_lo"], KC)
                pe.wait_ge(S["c16"], NT)
                pe.wait_ge(S["item_lo"], len(items))
            if t == 4:
                pe.wait_ge(S["q_lo"], 2 * KC)
            if t >= 2:
                pe.wait_ge(S["masked"], t - 1)
            for n in range(2):
                for k in range(KC):
                    m = three(bank(2 * (t % 2) + n), lambda a: qh[:, t, a, k * P:(k + 1) * P],
                              lambda a: kT[:, a, k, n * HALF:(n + 1) * HALF], k == 0, k == KC - 1)
            m.then_inc(S["s_ps"], 1)

        def p_turn(t):
            pe.wait_ge(S["exp_done"], t + 1)
            if t == 0:
                pe.wait_ge(S["q_lo"], 2)
            if t >= 1:
                pe.wait_ge(S["p_lo"], t)
            for k in range(NT):
                m = pe.transpose(ps[:, 4 + k // 4, (k % 4) * P:(k % 4 + 1) * P], T[:, t % 2, k * P:(k + 1) * P],
                                 ident[:, :])
            m.then_inc(S["pT_ps"], 1)

        def weighted_v(t):
            pe.wait_ge(S["p_lo"], t + 1)
            if t == 0:
                pe.wait_ge(S["q_lo"], 2 * KC)
            if t >= 1:
                pe.wait_ge(S["x1_ready"], t)
            for k in range(NT):
                m = three(bank(6), lambda a: pT[:, t % 2, a, k, :], lambda a: v[:, k, a, :], k == 0, k == NT - 1)
            m.then_inc(S["pv_ps"], 1)

        def h2_turn(t):
            pe.wait_ge(S["h2_ready"], t + 1)
            if t >= 1:
                pe.wait_ge(S["h1_tmp"], t)
            for k in range(KC):
                m = pe.transpose(bank(7)[:, k * P:(k + 1) * P], ht[:, k * P:(k + 1) * P], ident[:, :])
            m.then_inc(S["h2T_ps"], 1)

        def times_w1(t):
            pe.wait_ge(S["h2T_lo"], t + 1)
            if t == 0:
                pe.wait_ge(S["w_lo"], 4 * LOADS)
            for k in range(KC):
                m = three(bank(7), lambda a: hnT[:, a, k * P:(k + 1) * P], lambda a: wB[:, a, k, :],
                          k == 0, k == KC - 1)
            m.then_inc(S["w1_ps"], 1)

        pe.wait_ge(S["flag_ready"], 1)
        large = pe.value_load(flag[0:1, 0:1], min_val=0, max_val=1)
        pe.sem_inc(S["res_used"], 1)

        def rest_of_counts(g, product):
            with pe.If(large > 0):
                with pe.Fori(0, NT) as d:
                    pe.wait_ge(S["res_ready"], d + g * NT + 1)
                    product(1, d)
                    product(0, d).then_inc(S["res_used"], 1)

        def agg1(groups, ds):
            for g in groups:
                c, n = divmod(g, 2)
                for d in ds:
                    if g == 0:
                        pe.wait_ge(S["h1_lo"], d + 1)
                        if d in ACT_COUNTS:
                            pe.wait_ge(S["cnt_act"], ACT_COUNTS.index(d) + 1)
                        else:
                            pe.wait_ge(S["cnt_dve"], DVE_COUNTS.index(d) + 1)
                    for a in (1, 0):
                        last = d == NT - 1 and a == 0
                        if last:
                            rest_of_counts(g, lambda a, d: pe.matmul(bank(g), res_h[:, a, :], res[:, :], start=False,
                                                                     stop=False, skip_group_check=True))
                        m = pe.matmul(bank(g), qh[:, d, a, c * P:(c + 1) * P],
                                      cnt[:, d, n * HALF:(n + 1) * HALF], start=(d == 0 and a == 1), stop=last)
                if NT - 1 in ds:
                    m.then_inc(S["agg1_ps"], 1)

        for i in range(NT):
            scores(i)
            if i == 0:
                q_product(KC)
                q_product(KC + 1)
            if i >= 2:
                h2_turn(i - 2)
            if i >= 1:
                p_turn(i - 1)
            if i == 1:
                q_product(KC + 2)
                q_product(KC + 3)
            if i >= 2:
                times_w1(i - 2)
            if i >= 1:
                weighted_v(i - 1)
        pe.wait_ge(S["masked"], NT - 1)
        agg1((0, 1), range(0, NT - 2))
        h2_turn(NT - 2)
        p_turn(NT - 1)
        times_w1(NT - 2)
        weighted_v(NT - 1)
        pe.wait_ge(S["masked"], NT)
        agg1((2, 3), range(0, NT - 2))
        h2_turn(NT - 1)
        pe.wait_ge(S["diag_ready"], 1)
        pe.wait_ge(S["p_lo"], NT)
        for n in range(2):
            m = pe.matmul(bank(4 + n), ones[:, :], T[:, 0, n * HALF:(n + 1) * HALF], start=True, stop=True)
        m.then_inc(S["bc_ps"], 1)
        agg1((0, 1, 2, 3), range(NT - 2, NT - 1))
        times_w1(NT - 1)
        pe.wait_ge(S["bc_ready"], 1)
        agg1((4, 5), range(0, NT - 1))
        agg1((0, 1, 2, 3, 4, 5), range(NT - 1, NT))
        pe.wait_ge(S["h1_tmp"], NT)
        agg1((6, 7), range(0, NT))

        def times_w2(t, ks):
            if 0 in ks:
                pe.wait_ge(S["g_ready"], t + 1)
            for k in ks:
                m = three(bank(t), lambda a: zT[:, a, k, t * P:(t + 1) * P], lambda a: w2[:, a, k, :],
                          k == 0, k == KC - 1)
            if KC - 1 in ks:
                m.then_inc(S["w2_ps"], 1)

        pe.wait_ge(S["w_lo"], 5 * LOADS)
        for k in range(2):
            pe.wait_ge(S["z_lo"], k + 1)
            for t in range(6):
                times_w2(t, (k,))
        for t in range(6, NT):
            times_w2(t, (0, 1))
        for k in range(2, KC):
            pe.wait_ge(S["z_lo"], k + 1)
            for t in range(NT):
                times_w2(t, (k,))

        def agg2(t, ds):
            for d in ds:
                if t == 0:
                    pe.wait_ge(S["h2b_lo"], d + 1)
                for a in (1, 0):
                    last = d == NT - 1 and a == 0
                    if last:
                        rest_of_counts(2 * KC + t, lambda a, d: pe.matmul(
                            bank(t), res[:, 0:P], qh[:, bass.ds(d, 1), a, :].rearrange("p t n -> p (t n)"),
                            start=False, stop=False, skip_group_check=True))
                    m = pe.matmul(bank(t), cnt[:, d, t * P:(t + 1) * P], qh[:, d, a, :],
                                  start=(d == 0 and a == 1), stop=last)
            if NT - 1 in ds:
                m.then_inc(S["agg2_ps"], 1)

        pe.wait_ge(S["h2b_tmp"], 4)
        for d in range(NT):
            for t in range(4):
                agg2(t, (d,))
        for t in range(4, NT):
            agg2(t, range(NT))

    ctx.close()


_INS = ["x", "src", "dst", "L0_gnn_Wq", "L0_gnn_bq", "L0_gnn_Wk", "L0_gnn_bk", "L0_gnn_Wv", "L0_gnn_bv",
        "L1_gnn_W1", "L1_gnn_b1", "L1_gnn_gamma", "L1_gnn_beta", "L1_gnn_W2", "L1_gnn_b2"]


def kernel(**inputs):
    import numpy as np
    import concourse.bacc as bacc
    from concourse.bass_utils import run_bass_kernel_spmd

    nc = bacc.Bacc("TRN2", target_bir_lowering=False, num_devices=1, dynamic_dma_scratch_size=1024)
    arrays, args = {}, []
    for name in _INS:
        a = np.ascontiguousarray(inputs[name])
        arrays[name + "_in"] = a
        args.append(nc.dram_tensor(name + "_in", a.shape, mybir.dt.from_np(a.dtype), kind="ExternalInput").ap())
    args.append(nc.dram_tensor("out_0", (N, D), F32, kind="ExternalOutput").ap())
    gnn_kernel(nc, *args)
    r = run_bass_kernel_spmd(nc, [arrays], core_ids=[0])
    return r.results[0]["out_0"]
```

```python
from contextlib import ExitStack

import concourse.bass as bass
from concourse import mybir

P = 128
N = 1024
D = 512
E = 16384
NT = N // P
KC = D // P
NCH = E // P
HALF = 512
UNROLL = 4
RING = 4
BLOCKS = (7, 0, 1, 2, 3, 4, 5, 6)
QUOTAS = (3, 2, 2, 2, 2, 2, 2, 1)
TURNS = ((0, 1, 2, 3), (4, 5), (6, 7))
KV_BANKS = 3
LOADS = 2
XT = 4
EXACT = 4096.0
SCALE = float(D) ** -0.5
NEG = -1.0e6
EPS = 1e-5

ALU = mybir.AluOpType
ACT = mybir.ActivationFunctionType
AX = mybir.AxisListType
F32 = mybir.dt.float32
F32R = mybir.dt.float32r
BF16 = mybir.dt.bfloat16
F16 = mybir.dt.float16
I32 = mybir.dt.int32
I16 = mybir.dt.int16
U8 = mybir.dt.uint8


def gnn_kernel(nc, x, src, dst, Wq, bq, Wk, bk, Wv, bv, W1, b1, gamma, beta, W2, b2, out):
    ctx = ExitStack()

    def sb(name, shape, dt, where=ctx):
        return where.enter_context(nc.sbuf_tensor(name, shape, dt))

    def shared(*groups):
        made = []
        for g in groups:
            s = ExitStack()
            made += [sb(name, shape, dt, s) for name, shape, dt in g]
            s.close()
        return made

    def hold(name, kib):
        sb(name, [P, 256 * kib], F32)

    hT, pT, w2, _, w2_raw, g32 = shared(
        [("hT", [P, 2, KC, N], F32R)],
        [("pT", [P, 2, 2, NT, P], F32R), ("w2", [P, 2, KC, D], F32R)],
        [("pT_place", [P, 2, 2, NT, P], F32R), ("w2_raw", [P, 2, KC, D], F32)],
        [("g32", [P, KC, N], F32)])
    hold("region_hT", 32)
    wA, wA_raw, x1 = shared([("wA", [P, 2, KC, D], F32R)],
                            [("wA_raw", [P, 2, KC, D], F32)],
                            [("x1", [P, NT, D], F32)])
    hold("region_wA", 16)
    wB, wB_raw = shared([("wB", [P, 2, KC, D], F32R)], [("wB_raw", [P, 2, KC, D], F32)])
    hold("region_wB", 16)
    qh, src_oh, edge_i, edge_f = shared(
        [("qh", [P, NT, 2, KC * P], F32R)],
        [("src_oh", [P, RING, UNROLL, N], BF16)],
        [("edge_i", [P, 2, P], I32), ("edge_f", [P, 2, P], F32)])
    hold("region_qh", 32)
    kT, cnt = shared([("kT", [P, 2, KC, N], F32R)], [("cnt", [P, NT, N], F32R)])
    hold("region_kT", 32)
    v, zT = shared([("v", [P, NT, 2, D], F32R)], [("zT", [P, 2, KC, N], F32R)])
    hold("region_v", 32)
    T = sb("T", [P, 2, N], F32)
    cnt16 = sb("cnt16", [P, NT, N], I16)
    adj = sb("adj", [P, NT, N], U8)
    xt = sb("xt", [P, XT, D], F32)
    ht, iota = shared([("ht", [P, D], F32)], [("iota", [P, N], F16)])
    hold("region_ht", 2)
    dst_oh = sb("dst_oh", [P, RING, UNROLL, P], BF16)
    ecol = sb("ecol", [P, 2, NCH + UNROLL], F32)
    hnT, res, res_h, adjT = shared(
        [("hnT", [P, 2, KC * P], F32R)],
        [("res", [P, HALF], F32R), ("res_h", [P, 2, P], F32R)],
        [("adjT", [P, 2, N], BF16)])
    hold("region_hnT", 4)
    vb = sb("vb", [P, 2, D], F32)
    bias_row = sb("bias_row", [P, 2, D], F32)
    ident = sb("ident", [P, P], F32)
    identb = sb("identb", [P, P], BF16)
    zerob = sb("zerob", [P, P], BF16)
    half_pow = sb("half_pow", [P, NT], F32)
    bcol = sb("bcol", [P, 4, KC], F32)
    blk0 = sb("blk0", [P, NT], F32)
    chunk1 = sb("chunk1", [P, 2], F32)
    ext = sb("ext", [P, 2], F32)
    hit = sb("hit", [P, 3, NT], F32)
    span = sb("span", [P, 2, NT], F32)
    spanr = sb("spanr", [P, 2, NT], F32)
    lim = sb("lim", [P, 2, NT], F32)
    lohi = sb("lohi", [1, 2 * NT], I32)
    lsum = sb("lsum", [P, 2, NT], F32)
    lnc = sb("lnc", [P, 4, NT], F32)
    deg = sb("deg", [P, NT], F32)
    dinv = sb("dinv", [P, NT], F32)
    degm = sb("degm", [P, 3], F32)
    flag = sb("flag", [1, 1], I32)
    smx = sb("smx", [P, 4, NT], F32)
    bnst = sb("bnst", [P, 2, 6], F32)
    bnag = sb("bnag", [P, NT, 2], F32)
    lnb = sb("lnb", [P, 3, NT], F32)
    bnc = sb("bnc", [P, 4, KC], F32)

    ps = ctx.enter_context(nc.psum_tensor("ps", [P, 8, HALF], F32))
    bank = lambda b: ps[:, b, :]

    sem_names = """
    ident_zeroed ident_ready zeros_ready pad_ready iota_ready consts
    edges_in edge_f_ready ecol_ps ecol_ready span_ready span_max bounds_ready
    x_in0 x_in1 x_in2 x_in3 bcol_in bias_in b1_in
    wA_in0 wA_in1 wB_in0 wB_in1 w2_in0 w2_in1 w_hi wk_lo w_lo
    ln_sum ln_mean ln_sq ln_coef h_ready hT_ps hT_hi hT_lo hT_half_used
    onehots onehots_used c_done c16 adjT_ready adj_ps adj_evac
    kv_ps item_raw item_biased item_hi item_lo
    flag_max flag_ready dinv_ready q_ps q_hi q_lo
    s_ps mask_set masked top_ready exp_done rinv_ready pT_ps p_hi p_lo pv_ps x1_ready
    bn_ready ln2_coef h2_ready h2T_ps h2T_hi h2T_lo w1_ps h1_tmp h1_hi h1_lo
    cnt_act cnt_dve bc_ps bc_ready agg1_ps g_ready g_stats z_coef z_ready z_hi z_lo
    w2_ps h2b_tmp h2b_hi h2b_lo agg2_ps out_ready out_done0 out_done1 out_done2 out_done3
    res_ready res_used pool_step dve_step
    """.split()
    S = {n: ctx.enter_context(nc.semaphore(n)) for n in sem_names}

    kv = [("k", n, c) if what == "k" else ("v", KC * n + c, 0) for n in range(2) for what in "kv" for c in range(KC)]
    behind = [kv[sum(QUOTAS[:i]):sum(QUOTAS[:i + 1])] for i in range(NT)]
    kv_bank = lambda item: 5 + kv.index(item) % KV_BANKS
    EARLY = len(TURNS[0])
    items = []
    for i in range(NT):
        items += [("h", t, 0) for t in (TURNS[i] if 0 < i < len(TURNS) else ())] + behind[i]
    nth = lambda item: items.index(item) + 1
    turn_bank = lambda t: (2, 3, 5, 6)[t] if t < EARLY else 2 + t % 2
    q_bank = lambda g: (2, 6, 7, 5, 4, 7, 6, 7)[g]
    adj_bank = lambda i: 4 - i % 2

    def item_dest(item, part):
        what, n, c = item
        if what == "h":
            return hT[:, part, :, n * P:(n + 1) * P]
        return kT[:, part, c, n * HALF:(n + 1) * HALF] if what == "k" else v[:, n, part, :]

    weights = [(Wk, wA, wA_raw, "wA_in", 16), (Wv, wB, wB_raw, "wB_in", 16), (Wq, wA, wA_raw, "wA_in", 32),
               (W1, wB, wB_raw, "wB_in", 32), (W2, w2, w2_raw, "w2_in", 16)]

    def weight_load(i, j, what):
        k = KC // LOADS
        w, raw = weights[i][1:3]
        at, part = {"hi": (w, 0), "lo": (w, 1), "raw": (raw, 1)}[what]
        return at[:, part, j * k:(j + 1) * k, :]

    ACT_COUNTS, DVE_COUNTS = (0, 1, 2, 3), (4, 5, 6, 7)
    SPLIT_Q = next(i for i in range(NT) if kv[-KC - 1] in behind[i])

    block = ctx.enter_context(nc.Block())

    @block.sync
    def _(sp):
        sp.dma_start(edge_i[:, 0, :], dst.rearrange("(c j) -> c j", j=P)).then_inc(S["edges_in"], 16)
        sp.dma_start(edge_i[:, 1, :], src.rearrange("(c j) -> c j", j=P)).then_inc(S["edges_in"], 16)

        def load_x(n):
            if XT <= n < NT + XT:
                sp.wait_ge(S["h_ready"], n - XT + 1)
            if n >= NT + XT:
                sp.wait_ge(S["x1_ready"], n - NT - XT + 1)
            sp.dma_start(xt[:, n % XT, :], x[(n % NT) * P:(n % NT + 1) * P, :]).then_inc(S[f"x_in{n % XT}"], 16)

        def load_w(i):
            k = KC // LOADS
            for j in range(LOADS):
                sp.dma_start(weight_load(i, j, "raw"), weights[i][0].rearrange("(k p) n -> p k n", p=P)[
                    :, j * k:(j + 1) * k, :]).then_inc(S[f"{weights[i][3]}{j}"], 16)

        for t in range(XT):
            load_x(t)
        load_w(0)
        for i, b in enumerate((bq, bk, gamma, beta)):
            sp.dma_start(bcol[:, i, :], b.rearrange("(c p) -> p c", p=P),
                         allow_slow_non_contiguous=True).then_inc(S["bcol_in"], 16)
        load_w(1)
        sp.dma_start(bias_row[:, 0, :], bv.rearrange("(o n) -> o n", o=1).to_broadcast([P, D])).then_inc(S["bias_in"], 16)
        sp.dma_start(bias_row[:, 1, :], b1.rearrange("(o n) -> o n", o=1).to_broadcast([P, D])).then_inc(S["b1_in"], 16)
        for t in range(XT, NT):
            load_x(t)
        for t in range(XT):
            load_x(NT + t)
        sp.wait_ge(S["kv_ps"], kv.index(("k", 1, KC - 1)) + 1)
        load_w(2)
        sp.wait_ge(S["kv_ps"], len(kv))
        load_w(3)
        sp.wait_ge(S["item_biased"], NT)
        sp.dma_start(bias_row[:, 0, :], b2.rearrange("(o n) -> o n", o=1).to_broadcast([P, D])).then_inc(S["bias_in"], 16)
        sp.wait_ge(S["q_ps"], 2 * KC)
        load_w(4)
        for t in range(XT, NT):
            load_x(NT + t)
        for t in range(NT):
            sp.wait_ge(S["out_ready"], t + 1)
            sp.dma_start(out[t * P:(t + 1) * P, :], xt[:, t % XT, :]).then_inc(S[f"out_done{t % XT}"], 16)
        for u in range(XT):
            sp.wait_ge(S[f"out_done{u}"], 16 * NT // XT)

    @block.gpsimd
    def _(pool):
        def pw(out_, in_, w):
            return pool.tensor_tensor(out_, in_, half_pow[:, 0:w], ALU.pow)

        pool.memset(ident[:, :], 0.0).then_inc(S["ident_zeroed"], 1)
        pool.iota(blk0[:, :], pattern=[[P, NT]], base=0, channel_multiplier=0,
                  allow_small_or_imprecise_dtypes=True)
        pool.iota(chunk1[:, 0:1], pattern=[[0, 1]], base=1, channel_multiplier=1,
                  allow_small_or_imprecise_dtypes=True)
        pool.iota(chunk1[:, 1:2], pattern=[[0, 1]], base=NCH, channel_multiplier=-1,
                  allow_small_or_imprecise_dtypes=True).then_inc(S["iota_ready"], 1)
        pool.memset(zerob[:, :], 0.0).then_inc(S["zeros_ready"], 1)
        pool.wait_ge(S["ident_zeroed"], 1)
        pool.affine_select(out=ident[:, :], in_=ident[:, :], compare_op=ALU.not_equal, fill=1.0, base=0,
                           pattern=[[-1, P]], channel_multiplier=1).then_inc(S["ident_ready"], 1)
        pool.iota(iota[:, :], pattern=[[1, N]], base=0, channel_multiplier=0,
                  allow_small_or_imprecise_dtypes=True).then_inc(S["iota_ready"], 1)
        pool.memset(half_pow[:, :], -0.5)
        pool.wait_ge(S["ident_ready"], 1)
        pool.tensor_copy(identb[:, :], ident[:, :]).then_inc(S["consts"], 1)

        pool.wait_ge(S["span_ready"], 1)
        pool.partition_all_reduce(spanr[:, :, :].rearrange("p a b -> p (a b)"),
                                  span[:, :, :].rearrange("p a b -> p (a b)"), P,
                                  bass.bass_isa.ReduceOp.max).then_inc(S["span_max"], 1)

        n_steps = [0]

        def step(ins):
            n_steps[0] += 1
            ins.then_inc(S["pool_step"], 1)
            pool.wait_ge(S["pool_step"], n_steps[0])

        def ln1_mean(t):
            pool.wait_ge(S["ln_sum"], t + 1)
            pool.tensor_scalar(lnc[:, 0, t:t + 1], lsum[:, 0, t:t + 1], -1.0 / D, 0.0, ALU.mult,
                               ALU.add).then_inc(S["ln_mean"], 1)

        def ln1_coef(t):
            pool.wait_ge(S["ln_sq"], t + 1)
            step(pool.tensor_scalar(lnc[:, 1, t:t + 1], lsum[:, 1, t:t + 1], 1.0 / D, EPS, ALU.mult, ALU.add))
            step(pw(lnc[:, 2, t:t + 1], lnc[:, 1, t:t + 1], 1))
            pool.tensor_tensor(lnc[:, 3, t:t + 1], lnc[:, 0, t:t + 1], lnc[:, 2, t:t + 1],
                               ALU.mult).then_inc(S["ln_coef"], 1)

        def ln1(pair):
            for t in pair:
                ln1_mean(t)
            for t in pair:
                ln1_coef(t)

        def split_w(i, loads=range(LOADS)):
            for j in loads:
                pool.wait_ge(S["w_hi"], i * LOADS + j + 1)
                pool.tensor_tensor(weight_load(i, j, "lo"), weight_load(i, j, "raw"), weight_load(i, j, "hi").bitcast(F32),
                                   ALU.subtract).then_inc(S["w_lo"], 1)

        def split_item(item):
            i = nth(item)
            buf = vb[:, i % 2, :]
            if item[0] == "v":
                pool.wait_ge(S["item_raw"], i)
                pool.tensor_tensor(buf, buf, bias_row[:, 0, :], ALU.add).then_inc(S["item_biased"], 1)
            pool.wait_ge(S["item_hi"], i)
            if item[0] == "h":
                buf = buf.rearrange("p (k n) -> p k n", k=KC)
            pool.tensor_tensor(item_dest(item, 1), buf, item_dest(item, 0).bitcast(F32),
                               ALU.subtract).then_inc(S["item_lo"], 1)

        ln1((0, 1))
        ln1((2, 3))
        split_w(0, (1,))
        split_w(1)
        pool.wait_ge(S["bias_in"], 16)
        for i in range(NT):
            if 0 < i < len(TURNS):
                for t in TURNS[i]:
                    split_item(("h", t, 0))
            if i + 1 < len(TURNS):
                ln1(TURNS[i + 1])
            for item in behind[i]:
                split_item(item)
            if i == SPLIT_Q:
                split_w(2)
        pool.wait_ge(S["flag_max"], 1)
        pw(dinv[:, :], deg[:, :], NT).then_inc(S["dinv_ready"], 1)
        pool.partition_all_reduce(degm[:, 1:2], degm[:, 0:1], P,
                                  bass.bass_isa.ReduceOp.max).then_inc(S["flag_max"], 1)

        def mask_fill(t):
            if t >= 2:
                pool.wait_ge(S["pT_ps"], t - 1)
            pool.memset(T[:, t % 2, :], NEG / SCALE).then_inc(S["mask_set"], 1)

        def ln2_coef(t):
            pool.wait_ge(S["bn_ready"], t + 1)
            step(pool.tensor_scalar(lnb[:, 0, t:t + 1], bnag[:, t, 1:2], 1.0, EPS, ALU.mult, ALU.add))
            step(pw(lnb[:, 1, t:t + 1], lnb[:, 0, t:t + 1], 1))
            pool.tensor_scalar(lnb[:, 2, t:t + 1], bnag[:, t, 0:1], lnb[:, 1, t:t + 1], -1.0, ALU.mult,
                               ALU.mult).then_inc(S["ln2_coef"], 1)

        mask_fill(0)
        mask_fill(1)
        split_w(3)
        for t in range(NT):
            ln2_coef(t)
            if t + 2 < NT:
                mask_fill(t + 2)
            if 0 <= t - 1 < LOADS:
                split_w(4, (t - 1,))
        for c in range(KC):
            pool.wait_ge(S["g_stats"], c + 1)
            step(pool.tensor_scalar(bnc[:, 0, c:c + 1], bnag[:, c, 1:2], 1.0, EPS, ALU.mult, ALU.add))
            step(pw(bnc[:, 1, c:c + 1], bnc[:, 0, c:c + 1], 1))
            if c == 0:
                pool.wait_ge(S["bcol_in"], 64)
            step(pool.tensor_tensor(bnc[:, 2, c:c + 1], bnc[:, 1, c:c + 1], bcol[:, 2, c:c + 1], ALU.mult))
            step(pool.tensor_tensor(bnc[:, 0, c:c + 1], bnag[:, c, 0:1], bnc[:, 2, c:c + 1], ALU.mult))
            pool.tensor_tensor(bnc[:, 3, c:c + 1], bcol[:, 3, c:c + 1], bnc[:, 0, c:c + 1],
                               ALU.subtract).then_inc(S["z_coef"], 1)

    @block.scalar
    def _(act):
        def split_w(i, loads=range(LOADS)):
            for j in loads:
                act.wait_ge(S[f"{weights[i][3]}{j}"], weights[i][4])
                act.activation(weight_load(i, j, "hi"), weight_load(i, j, "raw"),
                               ACT.Copy).then_inc(S["w_hi"], 1)

        def hT_hi(t):
            act.wait_ge(S["hT_ps"], t + 1)
            act.activation(hT[:, 0, :, t * P:(t + 1) * P], bank(turn_bank(t)).rearrange("p (k n) -> p k n", k=KC),
                           ACT.Copy).then_inc(S["hT_hi"], 1)

        def adj_out(i):
            act.wait_ge(S["adj_ps"], i + 1)
            act.activation(adj[:, :, BLOCKS[i] * P:(BLOCKS[i] + 1) * P],
                           bank(adj_bank(i)).bitcast(BF16).rearrange("p (s n) -> p s n", s=NT),
                           ACT.Copy).then_inc(S["adj_evac"], 1)

        def layer_norms(pair):
            h = lambda t: T[:, (t % KC) // 2, (t % 2) * D:(t % 2 + 1) * D]
            for t in pair:
                act.wait_ge(S[f"x_in{t % XT}"], 16 * (t // XT + 1))
                if t >= KC:
                    act.wait_ge(S["hT_ps"], t - KC + 1)
                act.activation(h(t), xt[:, t % XT, :], ACT.Copy, accum_out=lsum[:, 0, t:t + 1]).then_inc(S["ln_sum"], 1)
            for t in pair:
                act.wait_ge(S["ln_mean"], t + 1)
                act.activation(h(t), xt[:, t % XT, :], ACT.Square, bias=lnc[:, 0, t:t + 1],
                               accum_out=lsum[:, 1, t:t + 1]).then_inc(S["ln_sq"], 1)
            for t in pair:
                act.wait_ge(S["ln_coef"], t + 1)
                act.activation(h(t), xt[:, t % XT, :], ACT.Relu, bias=lnc[:, 3, t:t + 1],
                               scale=lnc[:, 2, t:t + 1]).then_inc(S["h_ready"], 1)

        def counts(i):
            b = BLOCKS[i]
            act.wait_ge(S["c_done"], i + 1)
            act.activation(cnt16[:, b, :], ps[:, 0:2, :].rearrange("p a n -> p (a n)"), ACT.Copy,
                           accum_out=deg[:, b:b + 1]).then_inc(S["c16"], 1)

        def hi_of(item):
            i = nth(item)
            act.wait_ge(*((S["item_biased"], item[1] + 1) if item[0] == "v" else (S["item_raw"], i)))
            buf = vb[:, i % 2, :]
            if item[0] == "h":
                buf = buf.rearrange("p (k n) -> p k n", k=KC)
            act.activation(item_dest(item, 0), buf, ACT.Copy).then_inc(S["item_hi"], 1)

        late = []

        def take(item):
            what, n, c = item
            i = nth(item)
            act.wait_ge(S["hT_ps"], n + 1) if what == "h" else act.wait_ge(S["kv_ps"], kv.index(item) + 1)
            if i > 2:
                act.wait_ge(S["item_lo"], i - 2)
            if what == "k":
                ins = act.activation(vb[:, i % 2, :], bank(kv_bank(item)), ACT.Identity, bias=bcol[:, 1, c:c + 1])
            else:
                ins = act.activation(vb[:, i % 2, :], bank(turn_bank(n) if what == "h" else kv_bank(item)), ACT.Copy)
            ins.then_inc(S["item_raw"], 1)
            while late:
                hi_of(late.pop())
            if what == "v":
                late.append(item)
            else:
                hi_of(item)

        layer_norms((0, 1))
        split_w(0)
        layer_norms((2, 3))
        act.wait_ge(S["bcol_in"], 64)
        for i in range(NT):
            if i < len(TURNS):
                for t in TURNS[i]:
                    hT_hi(t) if t < EARLY else take(("h", t, 0))
            counts(i)
            if i == 0:
                split_w(1)
            if i + 1 < len(TURNS):
                layer_norms(TURNS[i + 1])
            if i >= 2:
                adj_out(i - 2)
            for item in behind[i]:
                take(item)
            while late:
                hi_of(late.pop())
            if i == SPLIT_Q:
                split_w(2)
        adj_out(NT - 2)
        adj_out(NT - 1)

        def q_hi(g):
            n, c = divmod(g, KC)
            act.wait_ge(S["q_ps"], g + 1)
            act.activation(qh[:, 4 * n:4 * n + 4, 0, c * P:(c + 1) * P], bank(q_bank(g)), ACT.Identity,
                           bias=bcol[:, 0, c:c + 1]).then_inc(S["q_hi"], 1)

        for g in range(KC + 1):
            q_hi(g)

        def softmax_exp(t):
            act.wait_ge(S["top_ready"], t + 1)
            act.activation(T[:, t % 2, :], T[:, t % 2, :], ACT.Exp, bias=smx[:, 1, t:t + 1], scale=SCALE,
                           accum_out=smx[:, 2, t:t + 1]).then_inc(S["exp_done"], 1)

        def p_hi(t):
            act.wait_ge(S["pT_ps"], t + 1)
            if t >= 2:
                act.wait_ge(S["pv_ps"], t - 1)
            act.activation(pT[:, t % 2, 0, :, :], ps[:, 4:6, :].rearrange("p a (k n) -> p (a k) n", n=P),
                           ACT.Copy).then_inc(S["p_hi"], 1)

        def h2_relu(t):
            act.wait_ge(S["ln2_coef"], t + 1)
            if t >= 1:
                act.wait_ge(S["h2T_ps"], t)
            act.activation(ht[:, :], x1[:, t, :], ACT.Relu, bias=lnb[:, 2, t:t + 1],
                           scale=lnb[:, 1, t:t + 1]).then_inc(S["h2_ready"], 1)

        def h2T_hi(t):
            act.wait_ge(S["h2T_ps"], t + 1)
            if t >= 1:
                act.wait_ge(S["w1_ps"], t)
            act.activation(hnT[:, 0, :], bank(7), ACT.Copy).then_inc(S["h2T_hi"], 1)

        def h1_hi(t):
            act.wait_ge(S["h1_tmp"], t + 1)
            act.activation(qh[:, t, 0, :], vb[:, t % 2, :], ACT.Copy, scale=dinv[:, t:t + 1]).then_inc(S["h1_hi"], 1)

        def count_parts(blocks):
            for b in blocks:
                act.activation(cnt[:, b, :], cnt16[:, b, :], ACT.Copy).then_inc(S["cnt_act"], 1)

        act.wait_ge(S["dinv_ready"], 1)
        for i in range(NT + 2):
            if i >= 2:
                h2_relu(i - 2)
                h2T_hi(i - 2)
            if i == 1:
                q_hi(KC + 2)
                act.wait_ge(S["hT_half_used"], 1)
            if 1 <= i <= NT:
                p_hi(i - 1)
            if i == 1:
                q_hi(KC + 3)
            if i == 0:
                q_hi(KC + 1)
            if i < NT:
                softmax_exp(i)
            if i == 0:
                split_w(3)
            if i == NT + 1:
                act.wait_ge(S["bc_ps"], 1)
                act.activation(T[:, 1, :], ps[:, 4:6, :].rearrange("p a n -> p (a n)"),
                               ACT.Copy).then_inc(S["bc_ready"], 1)
            if i >= 2:
                h1_hi(i - 2)
            if 0 <= i - 3 < LOADS:
                split_w(4, (i - 3,))
            if i == NT - 1:
                act.wait_ge(S["s_ps"], NT)
                count_parts(ACT_COUNTS)
        for c in range(KC):
            act.wait_ge(S["z_coef"], c + 1)
            act.activation(g32[:, c, :], g32[:, c, :], ACT.Relu, bias=bnc[:, 3, c:c + 1],
                           scale=bnc[:, 2, c:c + 1]).then_inc(S["z_ready"], 1)
            act.wait_ge(S["z_ready"], c + 1)
            act.activation(zT[:, 0, c, :], g32[:, c, :], ACT.Copy).then_inc(S["z_hi"], 1)
        for t in range(NT):
            act.wait_ge(S["h2b_tmp"], t + 1)
            act.activation(qh[:, t, 0, :], vb[:, t % 2, :], ACT.Copy, scale=dinv[:, t:t + 1]).then_inc(S["h2b_hi"], 1)

    @block.vector
    def _(dve):
        n_steps = [0]

        def step(ins):
            n_steps[0] += 1
            ins.then_inc(S["dve_step"], 1)
            dve.wait_ge(S["dve_step"], n_steps[0])

        dve.memset(ecol[:, :, NCH:], -1.0).then_inc(S["pad_ready"], 1)
        dve.wait_ge(S["edges_in"], 32)
        dve.tensor_copy(edge_f[:, :, :], edge_i[:, :, :]).then_inc(S["edge_f_ready"], 1)
        dve.wait_ge(S["edge_f_ready"], 1)
        dve.tensor_reduce(ext[:, 0:1], edge_f[:, 0, :], AX.X, ALU.min)
        step(dve.tensor_reduce(ext[:, 1:2], edge_f[:, 0, :], AX.X, ALU.max))
        dve.wait_ge(S["iota_ready"], 1)
        dve.tensor_scalar(hit[:, 0, :], blk0[:, :], ext[:, 1:2], None, ALU.is_le)
        step(dve.tensor_scalar(hit[:, 1, :], blk0[:, :], float(P - 1), ext[:, 0:1], ALU.add, ALU.is_ge))
        step(dve.tensor_tensor(hit[:, 2, :], hit[:, 0, :], hit[:, 1, :], ALU.mult))
        dve.tensor_scalar(span[:, 0, :], hit[:, 2, :], chunk1[:, 0:1], None, ALU.mult)
        dve.tensor_scalar(span[:, 1, :], hit[:, 2, :], chunk1[:, 1:2], None, ALU.mult).then_inc(S["span_ready"], 1)
        dve.wait_ge(S["ecol_ps"], 1)
        dve.tensor_copy(ecol[:, :, 0:NCH], bank(6)[:, 0:2 * P].rearrange("p (a n) -> p a n", a=2)).then_inc(S["ecol_ready"], 1)
        dve.wait_ge(S["span_max"], 1)
        step(dve.tensor_scalar(lim[0:1, 0, :], spanr[0:1, 1, :], -1.0, float(NCH), ALU.mult, ALU.add))
        step(dve.tensor_scalar(lim[0:1, 0, :], lim[0:1, 0, :], float(NCH - 1), None, ALU.min))
        step(dve.scalar_tensor_tensor(out=lim[0:1, 1, :], in0=lim[0:1, 0, :], scalar=1.0, in1=spanr[0:1, 0, :],
                                      op0=ALU.add, op1=ALU.max))
        dve.tensor_copy(lohi[0:1, :], lim[0:1, :, :].rearrange("p a b -> p (a b)")).then_inc(S["bounds_ready"], 1)
        dve.wait_ge(S["bounds_ready"], 1)
        dve.wait_ge(S["ecol_ready"], 1)

        def adj_cols(i):
            b = BLOCKS[i]
            dve.wait_ge(S["c16"], i + 1)
            if i >= 2:
                dve.wait_ge(S["adj_ps"], i - 1)
            dve.tensor_scalar(adjT[:, i % 2, :], cnt16[:, b, :], 1.0, None, ALU.min).then_inc(S["adjT_ready"], 1)
            dve.wait_ge(S["adjT_ready"], i + 1)
            dve.tensor_tensor(cnt16[:, b, b * P:(b + 1) * P], cnt16[:, b, b * P:(b + 1) * P], identb[:, :], ALU.add)

        def hT_lo(t):
            dve.wait_ge(S["hT_hi"], t + 1)
            dve.tensor_tensor(hT[:, 1, :, t * P:(t + 1) * P],
                              bank(turn_bank(t)).rearrange("p (k n) -> p k n", k=KC),
                              hT[:, 0, :, t * P:(t + 1) * P].bitcast(F32), ALU.subtract).then_inc(S["hT_lo"], 1)

        made = dve.alloc_register("made")
        dve.reg_mov(made, 0)
        dve.wait_ge(S["pad_ready"], 1)
        dve.wait_ge(S["iota_ready"], 2)
        dve.wait_ge(S["consts"], 1)
        for i, b in enumerate(BLOCKS):
            if i >= 2:
                adj_cols(i - 2)
            first = dve.value_load(lohi[0:1, b:b + 1], min_val=0, max_val=NCH - 1)
            end = dve.value_load(lohi[0:1, NT + b:NT + b + 1], min_val=1, max_val=NCH)
            with dve.Fori(first, end, UNROLL) as c:
                k = dve.snap(made, min_val=0, max_val=NT * NCH // UNROLL)
                slot = k & (RING - 1)
                dve.wait_ge(S["onehots_used"], k + 1)
                for j in range(UNROLL):
                    dve.tensor_scalar(src_oh[:, bass.ds(slot, 1), j, :].rearrange("p a n -> p (a n)"), iota[:, :],
                                      ecol[:, 1, bass.ds(c + j, 1)], None, ALU.is_equal)
                last = dve.tensor_tensor(
                    dst_oh[:, bass.ds(slot, 1), :, :].rearrange("p a j n -> p (a j) n"),
                    iota[:, b * P:(b + 1) * P].rearrange("p (o n) -> p o n", o=1).to_broadcast([P, UNROLL, P]),
                    ecol[:, 0, bass.ds(c, UNROLL)].rearrange("p (n o) -> p n o", o=1).to_broadcast(
                        [P, UNROLL, P]), ALU.is_equal)
                last.then_inc(S["onehots"], 1)
                dve.reg_add(made, made, 1)
            if i == 0:
                dve.wait_ge(S["w_hi"], 1)
                dve.tensor_tensor(weight_load(0, 0, "lo"), weight_load(0, 0, "raw"),
                                  weight_load(0, 0, "hi").bitcast(F32), ALU.subtract).then_inc(S["wk_lo"], 1)
                for t in TURNS[0]:
                    hT_lo(t)
        adj_cols(NT - 2)
        adj_cols(NT - 1)
        step(dve.tensor_scalar(deg[:, :], deg[:, :], 1.0, None, ALU.add))
        dve.tensor_reduce(degm[:, 0:1], deg[:, :], AX.X, ALU.max).then_inc(S["flag_max"], 1)
        dve.wait_ge(S["flag_max"], 1)
        dve.wait_ge(S["flag_max"], 2)
        step(dve.tensor_scalar(degm[0:1, 2:3], degm[0:1, 1:2], EXACT, None, ALU.is_gt))
        dve.tensor_copy(flag[0:1, 0:1], degm[0:1, 2:3]).then_inc(S["flag_ready"], 1)

        def q_lo(g):
            n, c = divmod(g, KC)
            at = lambda part: qh[:, 4 * n:4 * n + 4, part, c * P:(c + 1) * P]
            dve.wait_ge(S["q_hi"], g + 1)
            dve.scalar_tensor_tensor(out=at(1), in0=bank(q_bank(g)).rearrange("p (t n) -> p t n", t=4),
                                     scalar=bcol[:, 0, c:c + 1], in1=at(0).bitcast(F32), op0=ALU.add,
                                     op1=ALU.subtract).then_inc(S["q_lo"], 1)

        dve.wait_ge(S["bcol_in"], 64)
        for g in range(KC + 1):
            q_lo(g)

        def mask_and_max(t):
            dve.wait_ge(S["mask_set"], t + 1)
            dve.wait_ge(S["s_ps"], t + 1)
            dve.copy_predicated(T[:, t % 2, :], adj[:, t, :],
                                ps[:, 2 * (t % 2):2 * (t % 2) + 2, :].rearrange("p a n -> p (a n)")
                                ).then_inc(S["masked"], 1)
            dve.wait_ge(S["masked"], t + 1)
            step(dve.tensor_reduce(smx[:, 0, t:t + 1], T[:, t % 2, :], AX.X, ALU.max))
            dve.tensor_scalar(smx[:, 1, t:t + 1], smx[:, 0, t:t + 1], -SCALE, None, ALU.mult).then_inc(S["top_ready"], 1)

        def p_lo(t):
            dve.wait_ge(S["p_hi"], t + 1)
            dve.tensor_tensor(pT[:, t % 2, 1, :, :], ps[:, 4:6, :].rearrange("p a (k n) -> p (a k) n", n=P),
                              pT[:, t % 2, 0, :, :].bitcast(F32), ALU.subtract).then_inc(S["p_lo"], 1)
            dve.wait_ge(S["exp_done"], t + 1)
            dve.reciprocal(smx[:, 3, t:t + 1], smx[:, 2, t:t + 1]).then_inc(S["rinv_ready"], 1)

        def residual(t):
            n = NT + t
            dve.wait_ge(S[f"x_in{n % XT}"], 16 * (n // XT + 1))
            dve.wait_ge(S["rinv_ready"], t + 1)
            dve.wait_ge(S["pv_ps"], t + 1)
            dve.scalar_tensor_tensor(out=x1[:, t, :], in0=bank(6), scalar=smx[:, 3, t:t + 1], in1=xt[:, n % XT, :],
                                     op0=ALU.mult, op1=ALU.add).then_inc(S["x1_ready"], 1)
            dve.wait_ge(S["x1_ready"], t + 1)
            step(dve.bn_stats(bnst[:, 0, :], x1[:, t, :]))
            dve.bn_aggr(bnag[:, t, :], bnst[:, 0:1, :]).then_inc(S["bn_ready"], 1)
            dve.wait_ge(S["bn_ready"], t + 1)

        def h2T_lo(t):
            dve.wait_ge(S["h2T_hi"], t + 1)
            dve.tensor_tensor(hnT[:, 1, :], bank(7), hnT[:, 0, :].bitcast(F32), ALU.subtract).then_inc(S["h2T_lo"], 1)

        def h1_out(t):
            dve.wait_ge(S["w1_ps"], t + 1)
            dve.tensor_tensor(vb[:, t % 2, :], bank(7), bias_row[:, 1, :], ALU.add).then_inc(S["h1_tmp"], 1)
            dve.wait_ge(S["h1_hi"], t + 1)
            dve.scalar_tensor_tensor(out=qh[:, t, 1, :], in0=vb[:, t % 2, :], scalar=dinv[:, t:t + 1],
                                     in1=qh[:, t, 0, :].bitcast(F32), op0=ALU.mult,
                                     op1=ALU.subtract).then_inc(S["h1_lo"], 1)

        dve.wait_ge(S["b1_in"], 16)
        for i in range(NT + 2):
            if i >= 2:
                h2T_lo(i - 2)
            if i == 1:
                q_lo(KC + 2)
            if 1 <= i <= NT:
                p_lo(i - 1)
            if i == 1:
                q_lo(KC + 3)
            if i == 0:
                q_lo(KC + 1)
            if i < NT:
                mask_and_max(i)
            if i >= 2:
                h1_out(i - 2)
            if i == NT - 1:
                for b in DVE_COUNTS:
                    dve.tensor_copy(cnt[:, b, :], cnt16[:, b, :]).then_inc(S["cnt_dve"], 1)
            if 1 <= i <= NT:
                residual(i - 1)

        def z_lo(c):
            dve.wait_ge(S["z_hi"], c + 1)
            dve.tensor_tensor(zT[:, 1, c, :], g32[:, c, :], zT[:, 0, c, :].bitcast(F32),
                              ALU.subtract).then_inc(S["z_lo"], 1)

        dve.wait_ge(S["flag_ready"], 1)
        large = dve.value_load(flag[0:1, 0:1], min_val=0, max_val=1)

        def rest_of_counts(g, cols, h_cols=None):
            with dve.If(large > 0):
                with dve.Fori(0, NT) as d:
                    dve.wait_ge(S["res_used"], d + g * NT + 1)
                    w = cols.stop - cols.start
                    if h_cols:
                        dve.tensor_copy(res_h[:, :, :], qh[:, bass.ds(d, 1), :, h_cols].rearrange(
                            "p t a n -> p (t a) n").bitcast(F32))
                    dve.tensor_tensor(res[:, 0:w], cnt16[:, bass.ds(d, 1), cols].rearrange("p t n -> p (t n)"),
                                      cnt[:, bass.ds(d, 1), cols].rearrange("p t n -> p (t n)").bitcast(F32),
                                      ALU.subtract).then_inc(S["res_ready"], 1)

        dve.wait_ge(S["cnt_act"], len(ACT_COUNTS))
        dve.wait_ge(S["bc_ready"], 1)
        for c in range(KC):
            for n in range(2):
                g = 2 * c + n
                rest_of_counts(g, slice(n * HALF, (n + 1) * HALF), slice(c * P, (c + 1) * P))
                dve.wait_ge(S["agg1_ps"], g + 1)
                dve.tensor_tensor(g32[:, c, n * HALF:(n + 1) * HALF], bank(g),
                                  T[:, 1, n * HALF:(n + 1) * HALF], ALU.mult).then_inc(S["g_ready"], 1)
                dve.wait_ge(S["g_ready"], g + 1)
                step(dve.bn_stats(bnst[:, n, :], g32[:, c, n * HALF:(n + 1) * HALF]))
            dve.bn_aggr(bnag[:, c, :], bnst[:, :, :]).then_inc(S["g_stats"], 1)
            dve.wait_ge(S["g_stats"], c + 1)
            if c >= 1:
                z_lo(c - 1)
        z_lo(KC - 1)
        dve.wait_ge(S["bias_in"], 32)
        for t in range(NT + 1):
            if t < NT:
                dve.wait_ge(S["w2_ps"], t + 1)
                if t >= 2:
                    dve.wait_ge(S["h2b_lo"], t - 1)
                dve.tensor_tensor(vb[:, t % 2, :], bank(t), bias_row[:, 0, :], ALU.add).then_inc(S["h2b_tmp"], 1)
            if t >= 1:
                u = t - 1
                dve.wait_ge(S["h2b_hi"], u + 1)
                dve.scalar_tensor_tensor(out=qh[:, u, 1, :], in0=vb[:, u % 2, :], scalar=dinv[:, u:u + 1],
                                         in1=qh[:, u, 0, :].bitcast(F32), op0=ALU.mult,
                                         op1=ALU.subtract).then_inc(S["h2b_lo"], 1)
        for t in range(NT):
            rest_of_counts(2 * KC + t, slice(t * P, (t + 1) * P))
            dve.wait_ge(S["agg2_ps"], t + 1)
            if t >= XT:
                dve.wait_ge(S[f"out_done{t % XT}"], 16 * (t // XT))
            dve.scalar_tensor_tensor(out=xt[:, t % XT, :], in0=bank(t), scalar=dinv[:, t:t + 1],
                                     in1=x1[:, t, :], op0=ALU.mult, op1=ALU.add).then_inc(S["out_ready"], 1)

    @block.tensor
    def _(pe):
        def three(out_, stat, mov, first, last):
            pe.matmul(out_, stat(1), mov(0), start=first, stop=False)
            pe.matmul(out_, stat(0), mov(1), start=False, stop=False)
            return pe.matmul(out_, stat(0), mov(0), start=False, stop=last)

        pe.wait_ge(S["ident_ready"], 1)
        pe.wait_ge(S["edge_f_ready"], 1)
        for i in range(2):
            m = pe.transpose(bank(6)[:, i * P:(i + 1) * P], edge_f[:, i, :], ident[:, :])
        m.then_inc(S["ecol_ps"], 1)

        def hT_turn(t):
            pe.wait_ge(S["h_ready"], t + 1)
            if t == EARLY:
                pe.wait_ge(S["hT_lo"], EARLY)
            if t >= EARLY + 2:
                pe.wait_ge(S["item_raw"], nth(("h", t - 2, 0)))
            for k in range(KC):
                m = pe.transpose(bank(turn_bank(t))[:, k * P:(k + 1) * P],
                                 T[:, (t % KC) // 2, (t % 2) * D + k * P:(t % 2) * D + (k + 1) * P], ident[:, :])
            m.then_inc(S["hT_ps"], 1)

        def adj_turn(i):
            pe.wait_ge(S["adjT_ready"], i + 1)
            if i == 1:
                pe.wait_ge(S["item_raw"], nth(("h", NT - 1, 0)))
            if i >= 2:
                pe.wait_ge(S["adj_evac"], i - 1)
            for s in range(NT):
                m = pe.transpose(bank(adj_bank(i)).bitcast(BF16)[:, s * P:(s + 1) * P],
                                 adjT[:, i % 2, s * P:(s + 1) * P], identb[:, :])
            m.then_inc(S["adj_ps"], 1)

        pe.wait_ge(S["ecol_ready"], 1)
        pe.wait_ge(S["bounds_ready"], 1)
        pe.wait_ge(S["zeros_ready"], 1)
        pe.wait_ge(S["consts"], 1)
        pe.sem_inc(S["onehots_used"], RING)
        used = pe.alloc_register("used")
        pe.reg_mov(used, 0)

        def kv_product(item):
            what, n, c = item
            g = kv.index(item)
            if g == 0:
                pe.wait_ge(S["hT_lo"], EARLY)
                pe.wait_ge(S["wk_lo"], 1)
                pe.wait_ge(S["w_lo"], LOADS - 1)
            if item == ("v", 0, 0):
                pe.wait_ge(S["w_lo"], 2 * LOADS - 1)
            if item == ("k", 1, 0):
                pe.wait_ge(S["item_lo"], nth(("h", NT - 1, 0)))
            if g >= KV_BANKS:
                pe.wait_ge(S["item_raw"], nth(kv[g - KV_BANKS]))
            for k in range(KC):
                if what == "k":
                    m = three(bank(kv_bank(item)), lambda a: wA[:, a, k, c * P:(c + 1) * P],
                              lambda a: hT[:, a, k, n * HALF:(n + 1) * HALF], k == 0, k == KC - 1)
                else:
                    m = three(bank(kv_bank(item)), lambda a: hT[:, a, k, n * P:(n + 1) * P],
                              lambda a: wB[:, a, k, :], k == 0, k == KC - 1)
            m.then_inc(S["kv_ps"], 1)

        for i, b in enumerate(BLOCKS):
            if i >= 1:
                pe.wait_ge(S["c16"], i)
            for n in range(2):
                pe.matmul(ps[:, n, 0:32], zerob[:, :], zerob[:, 0:32], start=True, stop=False,
                          skip_group_check=True)
            first = pe.value_load(lohi[0:1, b:b + 1], min_val=0, max_val=NCH - 1)
            end = pe.value_load(lohi[0:1, NT + b:NT + b + 1], min_val=1, max_val=NCH)
            for t in TURNS[0][:2] if i == 0 else ():
                hT_turn(t)
            with pe.Fori(first, end, UNROLL):
                k = pe.snap(used, min_val=0, max_val=NT * NCH // UNROLL)
                slot = k & (RING - 1)
                pe.wait_ge(S["onehots"], k + 1)
                for j in range(UNROLL):
                    for n in range(2):
                        m = pe.matmul(ps[:, n, :], dst_oh[:, bass.ds(slot, 1), j, :].rearrange("p a n -> p (a n)"),
                                      src_oh[:, bass.ds(slot, 1), j, n * HALF:(n + 1) * HALF].rearrange(
                                          "p a n -> p (a n)"), start=False, stop=False, skip_group_check=True)
                m.then_inc(S["onehots_used"], 1)
                pe.reg_add(used, used, 1)
            for n in range(2):
                m = pe.matmul(ps[:, n, 0:32], zerob[:, :], zerob[:, 0:32], start=False, stop=True,
                              skip_group_check=True)
            m.then_inc(S["c_done"], 1)
            for t in (TURNS[0][2:], *TURNS[1:])[i] if i < len(TURNS) else ():
                hT_turn(t)
            if i >= 2:
                adj_turn(i - 2)
            for item in behind[i]:
                kv_product(item)
        adj_turn(NT - 2)
        adj_turn(NT - 1)

        def q_product(g):
            n, c = divmod(g, KC)
            if g == 0:
                pe.wait_ge(S["w_lo"], 3 * LOADS - 1)
                pe.wait_ge(S["item_lo"], nth(("h", NT - 1, 0)))
            if 1 <= g < KC:
                pe.wait_ge(S["item_raw"], nth(kv[g - KC]))
            if g == KC:
                pe.wait_ge(S["adj_evac"], NT - 1)
            if g > KC:
                pe.wait_ge(S["q_lo"], max(h for h in range(g) if q_bank(h) == q_bank(g)) + 1)
            for k in range(KC):
                m = three(bank(q_bank(g)), lambda a: wA[:, a, k, c * P:(c + 1) * P],
                          lambda a: hT[:, a, k, n * HALF:(n + 1) * HALF], k == 0, k == KC - 1)
                if (g, k) == (2 * KC - 1, KC // 2 - 1):
                    m.then_inc(S["hT_half_used"], 1)
            m.then_inc(S["q_ps"], 1)

        for g in range(KC + 1):
            q_product(g)

        def scores(t):
            if t == 0:
                pe.wait_ge(S["q_lo"], KC)
                pe.wait_ge(S["c16"], NT)
                pe.wait_ge(S["item_lo"], len(items))
            if t == 1:
                pe.wait_ge(S["adj_evac"], NT)
            if t >= 2:
                pe.wait_ge(S["masked"], t - 1)
            for n in range(2):
                for k in range(KC):
                    if (n, k) == (1, KC - 1) and t >= 2:
                        h2_turn(t - 2)
                    m = three(bank(2 * (t % 2) + n), lambda a: qh[:, t, a, k * P:(k + 1) * P],
                              lambda a: kT[:, a, k, n * HALF:(n + 1) * HALF], k == 0, k == KC - 1)
            m.then_inc(S["s_ps"], 1)

        def p_turn(t):
            pe.wait_ge(S["exp_done"], t + 1)
            if t == 0:
                pe.wait_ge(S["q_lo"], KC + 1)
            if t >= 1:
                pe.wait_ge(S["p_lo"], t)
            for k in range(NT):
                m = pe.transpose(ps[:, 4 + k // 4, (k % 4) * P:(k % 4 + 1) * P], T[:, t % 2, k * P:(k + 1) * P],
                                 ident[:, :])
            m.then_inc(S["pT_ps"], 1)

        def weighted_v(t):
            pe.wait_ge(S["p_lo"], t + 1)
            if t == 0:
                pe.wait_ge(S["q_lo"], 2 * KC - 1)
            if t >= 1:
                pe.wait_ge(S["x1_ready"], t)
            for k in range(NT):
                m = three(bank(6), lambda a: pT[:, t % 2, a, k, :], lambda a: v[:, k, a, :], k == 0, k == NT - 1)
            m.then_inc(S["pv_ps"], 1)

        def h2_turn(t):
            pe.wait_ge(S["h2_ready"], t + 1)
            if t == 0:
                pe.wait_ge(S["q_lo"], 2 * KC)
            if t >= 1:
                pe.wait_ge(S["h1_tmp"], t)
            for k in range(KC):
                m = pe.transpose(bank(7)[:, k * P:(k + 1) * P], ht[:, k * P:(k + 1) * P], ident[:, :])
            m.then_inc(S["h2T_ps"], 1)

        def times_w1(t):
            pe.wait_ge(S["h2T_lo"], t + 1)
            if t == 0:
                pe.wait_ge(S["w_lo"], 4 * LOADS - 1)
            for k in range(KC):
                m = three(bank(7), lambda a: hnT[:, a, k * P:(k + 1) * P], lambda a: wB[:, a, k, :],
                          k == 0, k == KC - 1)
            m.then_inc(S["w1_ps"], 1)

        pe.wait_ge(S["flag_ready"], 1)
        large = pe.value_load(flag[0:1, 0:1], min_val=0, max_val=1)
        pe.sem_inc(S["res_used"], 1)

        def rest_of_counts(g, product):
            with pe.If(large > 0):
                with pe.Fori(0, NT) as d:
                    pe.wait_ge(S["res_ready"], d + g * NT + 1)
                    product(1, d)
                    product(0, d).then_inc(S["res_used"], 1)

        def agg1(groups, ds):
            for g in groups:
                c, n = divmod(g, 2)
                for d in ds:
                    if g == 0:
                        pe.wait_ge(S["h1_lo"], d + 1)
                        if d in ACT_COUNTS:
                            pe.wait_ge(S["cnt_act"], ACT_COUNTS.index(d) + 1)
                        else:
                            pe.wait_ge(S["cnt_dve"], DVE_COUNTS.index(d) + 1)
                    for a in (1, 0):
                        last = d == NT - 1 and a == 0
                        if last:
                            rest_of_counts(g, lambda a, d: pe.matmul(bank(g), res_h[:, a, :], res[:, :], start=False,
                                                                     stop=False, skip_group_check=True))
                        m = pe.matmul(bank(g), qh[:, d, a, c * P:(c + 1) * P],
                                      cnt[:, d, n * HALF:(n + 1) * HALF], start=(d == 0 and a == 1), stop=last)
                if NT - 1 in ds:
                    m.then_inc(S["agg1_ps"], 1)

        for i in range(NT):
            scores(i)
            if i == 0:
                q_product(KC + 1)
            if i >= 1:
                p_turn(i - 1)
            if i == 1:
                q_product(KC + 2)
                q_product(KC + 3)
            if i >= 2:
                times_w1(i - 2)
            if i >= 1:
                weighted_v(i - 1)
        early = (0, 4, 1, 5, 2, 3)
        pe.wait_ge(S["masked"], NT - 1)
        agg1((0, 1), early)
        h2_turn(NT - 2)
        p_turn(NT - 1)
        times_w1(NT - 2)
        weighted_v(NT - 1)
        pe.wait_ge(S["masked"], NT)
        agg1((2, 3), early)
        h2_turn(NT - 1)
        pe.wait_ge(S["dinv_ready"], 1)
        pe.wait_ge(S["p_lo"], NT)
        for b in range(NT):
            m = pe.transpose(ps[:, 4 + b // 4, (b % 4) * P:(b % 4 + 1) * P],
                             dinv[:, b:b + 1].to_broadcast([P, P]), ident[:, :])
        m.then_inc(S["bc_ps"], 1)
        agg1((0, 1, 2, 3), range(NT - 2, NT - 1))
        times_w1(NT - 1)
        pe.wait_ge(S["bc_ready"], 1)
        agg1((4, 5), range(0, NT - 1))
        agg1((0, 1, 2, 3, 4, 5), range(NT - 1, NT))
        pe.wait_ge(S["h1_tmp"], NT)
        agg1((6, 7), range(0, NT))

        def times_w2(t, ks):
            if 0 in ks:
                pe.wait_ge(S["g_ready"], t + 1)
            for k in ks:
                m = three(bank(t), lambda a: zT[:, a, k, t * P:(t + 1) * P], lambda a: w2[:, a, k, :],
                          k == 0, k == KC - 1)
            if KC - 1 in ks:
                m.then_inc(S["w2_ps"], 1)

        pe.wait_ge(S["w_lo"], 5 * LOADS - 1)
        for k in range(2):
            pe.wait_ge(S["z_lo"], k + 1)
            for t in range(6):
                times_w2(t, (k,))
        for t in range(6, NT):
            times_w2(t, (0, 1))
        for k in range(2, KC):
            pe.wait_ge(S["z_lo"], k + 1)
            for t in range(NT):
                times_w2(t, (k,))

        def agg2(t, ds):
            for d in ds:
                if t == 0:
                    pe.wait_ge(S["h2b_lo"], d + 1)
                for a in (1, 0):
                    last = d == NT - 1 and a == 0
                    if last:
                        rest_of_counts(2 * KC + t, lambda a, d: pe.matmul(
                            bank(t), res[:, 0:P], qh[:, bass.ds(d, 1), a, :].rearrange("p t n -> p (t n)"),
                            start=False, stop=False, skip_group_check=True))
                    m = pe.matmul(bank(t), cnt[:, d, t * P:(t + 1) * P], qh[:, d, a, :],
                                  start=(d == 0 and a == 1), stop=last)
            if NT - 1 in ds:
                m.then_inc(S["agg2_ps"], 1)

        pe.wait_ge(S["h2b_tmp"], 4)
        for d in range(NT):
            for t in range(4):
                agg2(t, (d,))
        for t in range(4, NT):
            agg2(t, range(NT))

    ctx.close()


_INS = ["x", "src", "dst", "L0_gnn_Wq", "L0_gnn_bq", "L0_gnn_Wk", "L0_gnn_bk", "L0_gnn_Wv", "L0_gnn_bv",
        "L1_gnn_W1", "L1_gnn_b1", "L1_gnn_gamma", "L1_gnn_beta", "L1_gnn_W2", "L1_gnn_b2"]


def kernel(**inputs):
    import numpy as np
    import concourse.bacc as bacc
    from concourse.bass_utils import run_bass_kernel_spmd

    nc = bacc.Bacc("TRN2", target_bir_lowering=False, num_devices=1, dynamic_dma_scratch_size=1024)
    arrays, args = {}, []
    for name in _INS:
        a = np.ascontiguousarray(inputs[name])
        arrays[name + "_in"] = a
        args.append(nc.dram_tensor(name + "_in", a.shape, mybir.dt.from_np(a.dtype), kind="ExternalInput").ap())
    args.append(nc.dram_tensor("out_0", (N, D), F32, kind="ExternalOutput").ap())
    gnn_kernel(nc, *args)
    r = run_bass_kernel_spmd(nc, [arrays], core_ids=[0])
    return r.results[0]["out_0"]
```
